# Optimizing a Trainium2 kernel written in Bass

```python
import numpy as np
import jax
import jax.numpy as jnp

def _softmax(x, axis=-1):
    return jax.nn.softmax(x, axis=axis)

def _gelu(x):
    return jax.nn.gelu(x, approximate=True)

def _silu(x):
    return jax.nn.silu(x)

def _sigmoid(x):
    return jax.nn.sigmoid(x)

def _layernorm(x, axis=-1, eps=1e-05):
    m = jnp.mean(x, axis=axis, keepdims=True)
    v = jnp.var(x, axis=axis, keepdims=True)
    return (x - m) / jnp.sqrt(v + eps)

def _scatter_add(tgt, idx, src, axis=0):
    return tgt.at[idx].add(src)

def _segment_sum(src, seg, n):
    return jax.ops.segment_sum(src, seg, n)
kernel_name = 'mk_conv_seq_d4_conv_nhwc256_r4_2fbc25'

def setup_inputs(seed: int=0):
    np.random.seed(seed)
    _w = jnp.asarray

    def _rec_inputs():
        import jax
        import jax.numpy as jnp
        _gk = jax.random.key(seed)
        x = 7.22e-05 + 1 * jax.random.normal(jax.random.fold_in(_gk, 1), (8, 16, 16, 64), jnp.float32)
        return x
    x = _rec_inputs()

    def _L0_conv_setup():
        import jax, jax.numpy as jnp
        import numpy as np
        B, H, W, C = (8, 16, 16, 64)
        RC = C // 8
        key = jax.random.key(seed)
        ks = jax.random.split(key, 4)
        x = jax.random.normal(ks[0], (B, H, W, C), dtype=jnp.float32)
        wq = jax.random.normal(ks[1], (C, RC), dtype=jnp.float32) * (1.0 / np.sqrt(C))
        wk = jax.random.normal(ks[2], (C, RC), dtype=jnp.float32) * (1.0 / np.sqrt(C))
        wv = jax.random.normal(ks[3], (C, C), dtype=jnp.float32) * (1.0 / np.sqrt(C))
        bq = jnp.zeros((RC,), dtype=jnp.float32)
        bk = jnp.zeros((RC,), dtype=jnp.float32)
        bv = jnp.zeros((C,), dtype=jnp.float32)
        return {'x': x, 'wq': wq, 'bq': bq, 'wk': wk, 'bk': bk, 'wv': wv, 'bv': bv}
    _L0_conv_all = _L0_conv_setup()
    _L0_conv_in = {k: v for k, v in _L0_conv_all.items() if k in ('wq', 'bq', 'wk', 'bk', 'wv', 'bv')}
    del _L0_conv_all

    def _L1_conv_setup():
        import jax, jax.numpy as jnp
        import numpy as np
        EPS = 1e-06
        GROUPS = 32

        def group_norm(x, scale, bias):
            B, H, W, C = x.shape
            g = GROUPS
            xg = x.reshape(B, H, W, g, C // g)
            mean = jnp.mean(xg, axis=(1, 2, 4), keepdims=True)
            var = jnp.var(xg, axis=(1, 2, 4), keepdims=True)
            xg = (xg - mean) * jax.lax.rsqrt(var + EPS)
            return xg.reshape(B, H, W, C) * scale + bias

        def nin(x, w, b):
            return jnp.einsum('bhwc,cd->bhwd', x, w) + b
        key = jax.random.key(seed)
        ks = jax.random.split(key, 11)
        B, H, W, C = (8, 16, 16, 64)
        s = 1.0 / np.sqrt(C)
        return {'x': jax.random.normal(ks[0], (B, H, W, C), jnp.float32), 'gn_scale': jnp.ones((C,), jnp.float32), 'gn_bias': jnp.zeros((C,), jnp.float32), 'Wq': jax.random.normal(ks[1], (C, C), jnp.float32) * s, 'bq': jnp.zeros((C,), jnp.float32), 'Wk': jax.random.normal(ks[2], (C, C), jnp.float32) * s, 'bk': jnp.zeros((C,), jnp.float32), 'Wv': jax.random.normal(ks[3], (C, C), jnp.float32) * s, 'bv': jnp.zeros((C,), jnp.float32), 'Wo': jax.random.normal(ks[4], (C, C), jnp.float32) * s * 0.1, 'bo': jnp.zeros((C,), jnp.float32)}
    _L1_conv_all = _L1_conv_setup()
    _L1_conv_in = {k: v for k, v in _L1_conv_all.items() if k in ('gn_scale', 'gn_bias', 'Wq', 'bq', 'Wk', 'bk', 'Wv', 'bv', 'Wo', 'bo')}
    del _L1_conv_all

    def _L2_conv_setup():
        import jax, jax.numpy as jnp
        import numpy as np
        HEX_OFFSETS = [(0, 0), (1, 0), (-1, 0), (0, 1), (0, -1), (1, -1), (-1, 1)]
        NUM_NEIGHBORS = 7
        D_MODEL = 64
        NHEAD = 8
        DFF = 256
        EPS = 1e-05

        def _gather_hex(x):
            B, H, W, C = x.shape
            r = jnp.arange(H)[:, None]
            q = jnp.arange(W)[None, :]
            outs = []
            for dq, dr in HEX_OFFSETS:
                nq = q + dq
                nr = r + dr
                valid = (nq >= 0) & (nq < W) & (nr >= 0) & (nr < H)
                nq_c = jnp.where(valid, nq, 0)
                nr_c = jnp.where(valid, nr, 0)
                feat = x[:, nr_c, nq_c, :]
                outs.append(feat * valid[None, :, :, None].astype(x.dtype))
            return jnp.stack(outs, axis=3)

        def _layernorm(x, g, b):
            mu = jnp.mean(x, axis=-1, keepdims=True)
            var = jnp.mean(jnp.square(x - mu), axis=-1, keepdims=True)
            return (x - mu) * jax.lax.rsqrt(var + EPS) * g + b
        key = jax.random.key(seed)
        ks = jax.random.split(key, 12)
        B, H, W, C = (16, 16, 16, D_MODEL)
        s = 1.0 / np.sqrt(C)
        sf = 1.0 / np.sqrt(DFF)
        return {'src': jax.random.normal(ks[0], (B, H, W, C), dtype=jnp.float32), 'in_proj_w': jax.random.uniform(ks[1], (3 * C, C), minval=-s, maxval=s, dtype=jnp.float32), 'in_proj_b': jnp.zeros((3 * C,), dtype=jnp.float32), 'out_w': jax.random.uniform(ks[2], (C, C), minval=-s, maxval=s, dtype=jnp.float32), 'out_b': jnp.zeros((C,), dtype=jnp.float32), 'w1': jax.random.uniform(ks[3], (DFF, C), minval=-s, maxval=s, dtype=jnp.float32), 'b1': jax.random.uniform(ks[4], (DFF,), minval=-s, maxval=s, dtype=jnp.float32), 'w2': jax.random.uniform(ks[5], (C, DFF), minval=-sf, maxval=sf, dtype=jnp.float32), 'b2': jax.random.uniform(ks[6], (C,), minval=-sf, maxval=sf, dtype=jnp.float32), 'g1': jnp.ones((C,), dtype=jnp.float32), 'beta1': jnp.zeros((C,), dtype=jnp.float32), 'g2': jnp.ones((C,), dtype=jnp.float32), 'beta2': jnp.zeros((C,), dtype=jnp.float32)}
    _L2_conv_all = _L2_conv_setup()
    _L2_conv_in = {k: v for k, v in _L2_conv_all.items() if k in ('in_proj_w', 'in_proj_b', 'out_w', 'out_b', 'w1', 'b1', 'w2', 'b2', 'g1', 'beta1', 'g2', 'beta2')}
    del _L2_conv_all

    def _L3_conv_setup():
        import jax, jax.numpy as jnp
        import numpy as np
        from jax import lax
        EPS = 0.001
        DN = ('NHWC', 'HWIO', 'NHWC')

        def _bn(x, gamma, beta, mean, var):
            inv = gamma * lax.rsqrt(var + EPS)
            return x * inv + (beta - mean * inv)
        key = jax.random.key(seed)
        ks = jax.random.split(key, 5)
        B, H, W, C = (32, 56, 56, 64)
        G, CG = (32, 4)
        CM = G * CG
        x = jax.random.normal(ks[0], (B, H, W, C), jnp.float32)
        w1 = jax.random.normal(ks[1], (1, 1, C, CM), jnp.float32) * 0.05
        b1 = jnp.zeros((CM,), jnp.float32)
        g1 = jnp.ones((CM,), jnp.float32)
        be1 = jnp.zeros((CM,), jnp.float32)
        m1 = jnp.zeros((CM,), jnp.float32)
        v1 = jnp.ones((CM,), jnp.float32)
        w2 = jax.random.normal(ks[2], (3, 3, CG, CM), jnp.float32) * 0.1
        b2 = jnp.zeros((CM,), jnp.float32)
        g2 = jnp.ones((CM,), jnp.float32)
        be2 = jnp.zeros((CM,), jnp.float32)
        m2 = jnp.zeros((CM,), jnp.float32)
        v2 = jnp.ones((CM,), jnp.float32)
        w3 = jax.random.normal(ks[3], (1, 1, CM, C), jnp.float32) * 0.05
        b3 = jnp.zeros((C,), jnp.float32)
        return dict(x=x, w1=w1, b1=b1, g1=g1, be1=be1, m1=m1, v1=v1, w2=w2, b2=b2, g2=g2, be2=be2, m2=m2, v2=v2, w3=w3, b3=b3)
    _L3_conv_all = _L3_conv_setup()
    _L3_conv_in = {k: v for k, v in _L3_conv_all.items() if k in ('w1', 'b1', 'g1', 'be1', 'm1', 'v1', 'w2', 'b2', 'g2', 'be2', 'm2', 'v2', 'w3', 'b3')}
    del _L3_conv_all
    return {'x': x, 'L0_conv_wq': _L0_conv_in['wq'], 'L0_conv_bq': _L0_conv_in['bq'], 'L0_conv_wk': _L0_conv_in['wk'], 'L0_conv_bk': _L0_conv_in['bk'], 'L0_conv_wv': _L0_conv_in['wv'], 'L0_conv_bv': _L0_conv_in['bv'], 'L1_conv_gn_scale': _L1_conv_in['gn_scale'], 'L1_conv_gn_bias': _L1_conv_in['gn_bias'], 'L1_conv_Wq': _L1_conv_in['Wq'], 'L1_conv_bq': _L1_conv_in['bq'], 'L1_conv_Wk': _L1_conv_in['Wk'], 'L1_conv_bk': _L1_conv_in['bk'], 'L1_conv_Wv': _L1_conv_in['Wv'], 'L1_conv_bv': _L1_conv_in['bv'], 'L1_conv_Wo': _L1_conv_in['Wo'], 'L1_conv_bo': _L1_conv_in['bo'], 'L2_conv_in_proj_w': _L2_conv_in['in_proj_w'], 'L2_conv_in_proj_b': _L2_conv_in['in_proj_b'], 'L2_conv_out_w': _L2_conv_in['out_w'], 'L2_conv_out_b': _L2_conv_in['out_b'], 'L2_conv_w1': _L2_conv_in['w1'], 'L2_conv_b1': _L2_conv_in['b1'], 'L2_conv_w2': _L2_conv_in['w2'], 'L2_conv_b2': _L2_conv_in['b2'], 'L2_conv_g1': _L2_conv_in['g1'], 'L2_conv_beta1': _L2_conv_in['beta1'], 'L2_conv_g2': _L2_conv_in['g2'], 'L2_conv_beta2': _L2_conv_in['beta2'], 'L3_conv_w1': _L3_conv_in['w1'], 'L3_conv_b1': _L3_conv_in['b1'], 'L3_conv_g1': _L3_conv_in['g1'], 'L3_conv_be1': _L3_conv_in['be1'], 'L3_conv_m1': _L3_conv_in['m1'], 'L3_conv_v1': _L3_conv_in['v1'], 'L3_conv_w2': _L3_conv_in['w2'], 'L3_conv_b2': _L3_conv_in['b2'], 'L3_conv_g2': _L3_conv_in['g2'], 'L3_conv_be2': _L3_conv_in['be2'], 'L3_conv_m2': _L3_conv_in['m2'], 'L3_conv_v2': _L3_conv_in['v2'], 'L3_conv_w3': _L3_conv_in['w3'], 'L3_conv_b3': _L3_conv_in['b3']}

def reference(x, L0_conv_wq, L0_conv_bq, L0_conv_wk, L0_conv_bk, L0_conv_wv, L0_conv_bv, L1_conv_gn_scale, L1_conv_gn_bias, L1_conv_Wq, L1_conv_bq, L1_conv_Wk, L1_conv_bk, L1_conv_Wv, L1_conv_bv, L1_conv_Wo, L1_conv_bo, L2_conv_in_proj_w, L2_conv_in_proj_b, L2_conv_out_w, L2_conv_out_b, L2_conv_w1, L2_conv_b1, L2_conv_w2, L2_conv_b2, L2_conv_g1, L2_conv_beta1, L2_conv_g2, L2_conv_beta2, L3_conv_w1, L3_conv_b1, L3_conv_g1, L3_conv_be1, L3_conv_m1, L3_conv_v1, L3_conv_w2, L3_conv_b2, L3_conv_g2, L3_conv_be2, L3_conv_m2, L3_conv_v2, L3_conv_w3, L3_conv_b3):
    import jax
    import jax.numpy as jnp

    def _L0_conv_ref(x, wq, bq, wk, bk, wv, bv):
        import jax, jax.numpy as jnp
        import numpy as np
        B, H, W, C = (8, 16, 16, 64)
        RC = C // 8
        b, h, w, c = x.shape
        n = h * w
        q = jax.nn.relu(jnp.einsum('bhwc,cd->bhwd', x, wq) + bq).reshape(b, n, -1)
        k = jax.nn.relu(jnp.einsum('bhwc,cd->bhwd', x, wk) + bk).reshape(b, n, -1)
        v = (jnp.einsum('bhwc,cd->bhwd', x, wv) + bv).reshape(b, n, c)
        attn = jax.nn.softmax(jnp.einsum('bnd,bmd->bnm', q, k), axis=-1)
        out = jnp.einsum('bnm,bmc->bnc', attn, v).reshape(b, h, w, c)
        return out + x

    def _L1_conv_ref(x, gn_scale, gn_bias, Wq, bq, Wk, bk, Wv, bv, Wo, bo):
        import jax, jax.numpy as jnp
        import numpy as np
        EPS = 1e-06
        GROUPS = 32

        def group_norm(x, scale, bias):
            B, H, W, C = x.shape
            g = GROUPS
            xg = x.reshape(B, H, W, g, C // g)
            mean = jnp.mean(xg, axis=(1, 2, 4), keepdims=True)
            var = jnp.var(xg, axis=(1, 2, 4), keepdims=True)
            xg = (xg - mean) * jax.lax.rsqrt(var + EPS)
            return xg.reshape(B, H, W, C) * scale + bias

        def nin(x, w, b):
            return jnp.einsum('bhwc,cd->bhwd', x, w) + b
        B, H, W, C = x.shape
        h = group_norm(x, gn_scale, gn_bias)
        q = nin(h, Wq, bq)
        k = nin(h, Wk, bk)
        v = nin(h, Wv, bv)
        w = jnp.einsum('bhwc,bHWc->bhwHW', q, k) * C ** (-0.5)
        w = w.reshape(B, H, W, H * W)
        w = jax.nn.softmax(w, axis=-1)
        w = w.reshape(B, H, W, H, W)
        h = jnp.einsum('bhwHW,bHWc->bhwc', w, v)
        h = nin(h, Wo, bo)
        return x + h

    def _L2_conv_ref(src, in_proj_w, in_proj_b, out_w, out_b, w1, b1, w2, b2, g1, beta1, g2, beta2):
        import jax, jax.numpy as jnp
        import numpy as np
        HEX_OFFSETS = [(0, 0), (1, 0), (-1, 0), (0, 1), (0, -1), (1, -1), (-1, 1)]
        NUM_NEIGHBORS = 7
        D_MODEL = 64
        NHEAD = 8
        DFF = 256
        EPS = 1e-05

        def _gather_hex(x):
            B, H, W, C = x.shape
            r = jnp.arange(H)[:, None]
            q = jnp.arange(W)[None, :]
            outs = []
            for dq, dr in HEX_OFFSETS:
                nq = q + dq
                nr = r + dr
                valid = (nq >= 0) & (nq < W) & (nr >= 0) & (nr < H)
                nq_c = jnp.where(valid, nq, 0)
                nr_c = jnp.where(valid, nr, 0)
                feat = x[:, nr_c, nq_c, :]
                outs.append(feat * valid[None, :, :, None].astype(x.dtype))
            return jnp.stack(outs, axis=3)

        def _layernorm(x, g, b):
            mu = jnp.mean(x, axis=-1, keepdims=True)
            var = jnp.mean(jnp.square(x - mu), axis=-1, keepdims=True)
            return (x - mu) * jax.lax.rsqrt(var + EPS) * g + b
        B, H, W, C = src.shape
        nh, hd = (NHEAD, C // NHEAD)
        x = src
        kv = _gather_hex(x)
        wq, wk, wv = (in_proj_w[:C], in_proj_w[C:2 * C], in_proj_w[2 * C:])
        bq, bk, bv = (in_proj_b[:C], in_proj_b[C:2 * C], in_proj_b[2 * C:])
        qh = (x @ wq.T + bq).reshape(B, H, W, nh, hd)
        kh = (kv @ wk.T + bk).reshape(B, H, W, NUM_NEIGHBORS, nh, hd)
        vh = (kv @ wv.T + bv).reshape(B, H, W, NUM_NEIGHBORS, nh, hd)
        scale = 1.0 / np.sqrt(hd)
        scores = jnp.einsum('bxynd,bxyknd->bxynk', qh, kh) * scale
        attn = jax.nn.softmax(scores, axis=-1)
        ctx = jnp.einsum('bxynk,bxyknd->bxynd', attn, vh)
        attn_out = ctx.reshape(B, H, W, C) @ out_w.T + out_b
        x = _layernorm(x + attn_out, g1, beta1)
        ff = jax.nn.relu(x @ w1.T + b1) @ w2.T + b2
        x = _layernorm(x + ff, g2, beta2)
        return x

    def _L3_conv_ref(x, w1, b1, g1, be1, m1, v1, w2, b2, g2, be2, m2, v2, w3, b3):
        import jax, jax.numpy as jnp
        import numpy as np
        from jax import lax
        EPS = 0.001
        DN = ('NHWC', 'HWIO', 'NHWC')

        def _bn(x, gamma, beta, mean, var):
            inv = gamma * lax.rsqrt(var + EPS)
            return x * inv + (beta - mean * inv)
        h = lax.conv_general_dilated(x, w1, (1, 1), 'SAME', dimension_numbers=DN) + b1
        h = jax.nn.relu(_bn(h, g1, be1, m1, v1))
        h = lax.conv_general_dilated(h, w2, (1, 1), 'SAME', dimension_numbers=DN, feature_group_count=32) + b2
        h = jax.nn.relu(_bn(h, g2, be2, m2, v2))
        out = lax.conv_general_dilated(h, w3, (1, 1), 'SAME', dimension_numbers=DN) + b3
        return jax.nn.relu(out + x)

    def _gn(v, G=32, eps=1e-05):
        B_, H_, W_, C_ = v.shape
        g = v.reshape(B_, H_, W_, G, C_ // G)
        m = jnp.mean(g, axis=(1, 2, 4), keepdims=True)
        s = jnp.var(g, axis=(1, 2, 4), keepdims=True)
        return ((g - m) / jnp.sqrt(s + eps)).reshape(v.shape)

    def _ln_c(v, eps=1e-06):
        m = jnp.mean(v, axis=-1, keepdims=True)
        s = jnp.var(v, axis=-1, keepdims=True)
        return (v - m) / jnp.sqrt(s + eps)

    def _ln_t(v, eps=1e-05):
        m = jnp.mean(v, axis=-1, keepdims=True)
        s = jnp.var(v, axis=-1, keepdims=True)
        return (v - m) / jnp.sqrt(s + eps)

    def _to_tokens(v):
        B_, H_, W_, C_ = v.shape
        return v.reshape(B_, H_ * W_, C_)

    def _from_tokens(t, like):
        return t.reshape(like.shape)
    x = _L0_conv_ref(x, L0_conv_wq, L0_conv_bq, L0_conv_wk, L0_conv_bk, L0_conv_wv, L0_conv_bv)
    x = _L1_conv_ref(x, L1_conv_gn_scale, L1_conv_gn_bias, L1_conv_Wq, L1_conv_bq, L1_conv_Wk, L1_conv_bk, L1_conv_Wv, L1_conv_bv, L1_conv_Wo, L1_conv_bo)
    x = _L2_conv_ref(x, L2_conv_in_proj_w, L2_conv_in_proj_b, L2_conv_out_w, L2_conv_out_b, L2_conv_w1, L2_conv_b1, L2_conv_w2, L2_conv_b2, L2_conv_g1, L2_conv_beta1, L2_conv_g2, L2_conv_beta2)
    x = _L3_conv_ref(x, L3_conv_w1, L3_conv_b1, L3_conv_g1, L3_conv_be1, L3_conv_m1, L3_conv_v1, L3_conv_w2, L3_conv_b2, L3_conv_g2, L3_conv_be2, L3_conv_m2, L3_conv_v2, L3_conv_w3, L3_conv_b3)
    return x

_drawn_inputs = setup_inputs


def setup_inputs(seed=0):
    import zlib

    import numpy as np

    out = dict(_drawn_inputs(seed))
    spreads = {'L0_conv_bq': (0.0, 0.1),
     'L0_conv_bk': (0.0, 0.582),
     'L0_conv_bv': (0.0, 0.1),
     'L1_conv_gn_scale': (1.0, 0.6),
     'L1_conv_gn_bias': (0.0, 0.8),
     'L1_conv_bq': (0.0, 0.8),
     'L1_conv_bk': (0.0, 0.8),
     'L1_conv_bv': (0.0, 0.776),
     'L1_conv_bo': (0.0, 0.1),
     'L2_conv_in_proj_b': (0.0, 0.1),
     'L2_conv_out_b': (0.0, 0.1),
     'L2_conv_g1': (1.0, 0.2),
     'L2_conv_beta1': (0.0, 0.1),
     'L2_conv_g2': (1.0, 0.2),
     'L2_conv_beta2': (0.0, 0.1),
     'L3_conv_b1': (0.0, 0.49),
     'L3_conv_g1': (1.0, 0.6),
     'L3_conv_be1': (0.0, 0.525),
     'L3_conv_m1': (0.0, 0.546),
     'L3_conv_v1': (1.0, 0.6),
     'L3_conv_b2': (0.0, 0.1),
     'L3_conv_g2': (1.0, 0.6),
     'L3_conv_be2': (0.0, 0.1),
     'L3_conv_m2': (0.0, 0.1),
     'L3_conv_v2': (1.0, 0.6),
     'L3_conv_b3': (0.0, 0.1)}
    factors = {'L1_conv_Wq': 3.364, 'L1_conv_Wk': 3.202}
    for name, (base, spread) in spreads.items():
        noise = np.random.default_rng([zlib.crc32(name.encode()), seed]).standard_normal(out[name].shape)
        drawn = base * np.exp(spread * noise) if base else spread * noise
        out[name] = jnp.asarray(drawn.astype(out[name].dtype))
    for name, factor in factors.items():
        out[name] = (out[name] * factor).astype(out[name].dtype)
    return out
```

```python
from contextlib import ExitStack

import concourse.bass as bass
from concourse import mybir

F32 = mybir.dt.float32
ALU = mybir.AluOpType
ACT = mybir.ActivationFunctionType
AX = mybir.AxisListType

IMAGES, SIDE, CH = 8, 16, 64
TOK = SIDE * SIDE
PAIRS = IMAGES // 2
GROUPS = PAIRS // 2
BLK = TOK // 128
RC = CH // 8
HEADS, HD = 8, 8
DFF = 256
FH = DFF // 128
CM = 128
PAD = SIDE + 2
HEX_RUNS = [[(-1, 0), (0, 0), (1, 0)], [(0, -1), (0, 1)], [(1, -1), (-1, 1)]]
NB = sum(len(run) for run in HEX_RUNS)
EPS_GN, EPS_LN, EPS_BN = 1e-6, 1e-5, 1e-3

VEC64 = ["L1_conv_gn_scale", "L1_conv_gn_bias", "L1_conv_bq", "L1_conv_bk", "L1_conv_bv",
         "L0_conv_bv", "L1_conv_bo", "L2_conv_out_b", "L2_conv_b2",
         "L2_conv_g1", "L2_conv_beta1", "L2_conv_g2", "L2_conv_beta2", "L3_conv_b3"]
VEC128 = ["L3_conv_b1", "L3_conv_g1", "L3_conv_be1", "L3_conv_m1", "L3_conv_v1",
          "L3_conv_b2", "L3_conv_g2", "L3_conv_be2", "L3_conv_m2", "L3_conv_v2"]
ROW = {"L0_conv_bq": 0, "L0_conv_bk": 1}
for _name in VEC64 + VEC128:
    ROW[_name] = len(ROW)
ROW["in_proj_b"] = len(ROW)
ROW["L2_conv_b1"] = len(ROW) + 2
ROWS = ROW["L2_conv_b1"] + FH

BD = {n: k for k, n in enumerate(["L0_wv", "L1_Wq", "L1_Wk", "L1_Wv", "L1_Wo",
                                  "in_q", "in_k", "in_v", "out_w"])}


def build(nc, t, out):
    ctx = ExitStack()
    with ctx:
        def sb(name, *shape):
            return ctx.enter_context(nc.sbuf_tensor(name, list(shape), F32))

        def sem(name):
            return ctx.enter_context(nc.semaphore(name))

        bank = [ctx.enter_context(nc.psum_tensor(f"bank{i}", [128, 512], F32)) for i in range(6)]
        duo = ctx.enter_context(nc.psum_tensor("duo", [128, 1024], F32))
        S_BANK = [bank[0], bank[1]]
        T_BANK = [bank[2], bank[3]]
        O_BANK = bank[4]
        W_BANK = [bank[5][:, :], duo[:, 0:512], duo[:, 512:1024]]

        ident = sb("ident", 128, 128)
        centre = sb("centre", 128, 128)
        mean64 = sb("mean64", 128, 128)
        pairavg = sb("pairavg", 128, 128)
        head_sum = sb("head_sum", 128, 112 + 16 + 112)
        head_cast = sb("head_cast", 128, 2, PAIRS, 128)
        gmask = sb("gmask", 128, 128)
        epsln = sb("epsln", 128, 1)
        minus_half = sb("minus_half", 128, 4)
        zeros = sb("zeros", 128, 2 * PAD * PAD)
        k_mask = sb("k_mask", 128, 4)
        vrows = sb("vrows", ROWS, 128)
        vcol = sb("vcol", 128, ROWS)
        wbd = sb("wbd", 128, len(BD), 128)
        wqk0 = sb("wqk0", 128, 2, 64)
        wvT1 = sb("wvT1", 128, 128)
        wvo1 = sb("wvo1", 128, 128)
        inT = sb("inT", 128, 3, 128)
        outc = sb("outc", 128, 128)
        w1nat = sb("w1nat", 128, FH, 2, CH)
        w1T = sb("w1T", 128, 2, FH, 128)
        w2nat = sb("w2nat", CH, DFF)
        w2c = sb("w2c", 128, FH, CH)
        cb = sb("cb", 128, 3)
        qb8 = sb("qb8", 128, 1)
        c1 = sb("c1", 128, 2, CM)
        craw = sb("craw", 128, 9, CM)
        ctap = sb("ctap", 128, 9, CM)
        c3 = sb("c3", 128, CH)
        bnv = sb("bnv", 128, 2)
        bnr = sb("bnr", 128, 2)
        bninv = sb("bninv", 128, 2)
        bnsh = sb("bnsh", 128, 2)
        xin = sb("xin", 128, PAIRS, BLK, 2, CH)
        xT = sb("xT", 128, PAIRS, TOK)
        qk0 = sb("qk0", 128, GROUPS, 2, TOK)
        kz0 = sb("kz0", 128, IMAGES, TOK)
        v0 = sb("v0", 128, PAIRS * BLK, 128)
        prob = sb("prob", 128, 3, BLK, TOK)
        probn = sb("probn", 128, 2, BLK, TOK)
        probT = sb("probT", 128, 4, BLK, TOK)
        nmax = sb("nmax", 128, 2 * IMAGES, BLK)
        rsum = sb("rsum", 128, 2 * IMAGES, BLK)
        rrec = sb("rrec", 128, 2 * IMAGES, BLK)
        yT = sb("yT", 128, PAIRS, TOK)
        bnst = sb("bnst", 128, PAIRS, 6)
        mv = sb("mv", 128, PAIRS, 2)
        sq4 = sb("sq4", 128, PAIRS)
        gmv = sb("gmv", 128, PAIRS, 2)
        gvar = sb("gvar", 128, PAIRS)
        grs = sb("grs", 128, PAIRS)
        gsc = sb("gsc", 128, PAIRS)
        gbi = sb("gbi", 128, PAIRS)
        gtmp = sb("gtmp", 128, PAIRS)
        hT = sb("hT", 128, PAIRS, TOK)
        q1 = sb("q1", 128, PAIRS, TOK)
        kz1 = sb("kz1", 128, IMAGES, TOK)
        v1 = sb("v1", 128, PAIRS * BLK, 128)
        zT = sb("zT", 128, PAIRS, TOK)
        q2 = sb("q2", 128, PAIRS, TOK)
        k2 = sb("k2", 128, PAIRS, PAD, PAD)
        v2 = sb("v2", 128, PAIRS, PAD, PAD)
        qkprod = sb("qkprod", 128, 2, NB, TOK)
        smax = sb("smax", 128, 128)
        sexp = sb("sexp", 128, NB, 128)
        att = sb("att", 128, NB, 128)
        avprod = sb("avprod", 128, 2, NB, TOK)
        sq = sb("sq", 128, 2, 512)
        std = sb("std", 128, 2, 512)
        rstd = sb("rstd", 128, 2, 512)
        xhat = sb("xhat", 128, 2, 512)
        x1 = sb("x1", 128, GROUPS, 512)
        x2 = sb("x2", 128, GROUPS, 512)
        ffh = sb("ffh", 128, 2, FH, 2, 512)
        c1out = sb("c1out", 128, GROUPS, 2, 2, PAD, PAD)
        c2out = ffh[:, 0, :, :, :]
        x3 = std
        fin = xin

        x_in = [sem(f"x_in{g}") for g in range(GROUPS)]
        w_early = sem("w_early")
        w_late = sem("w_late")
        w_conv = sem("w_conv")
        stored = sem("stored")
        cleared = sem("cleared")
        id_ready = sem("id_ready")
        consts = sem("consts")
        pool_step = sem("pool_step")
        dve_step = sem("dve_step")
        act_step = sem("act_step")
        vrow_ps = sem("vrow_ps")
        vcol_ready = sem("vcol_ready")
        prep_ps = sem("prep_ps")
        prep_sb = sem("prep_sb")
        xT_ps, xT_sb = sem("xT_ps"), sem("xT_sb")
        qk0_ps, qk0_sb = sem("qk0_ps"), sem("qk0_sb")
        kz0_ready = sem("kz0_ready")
        v0_ps, v0_sb = sem("v0_ps"), sem("v0_sb")
        scores_ps = sem("scores_ps")
        max_ready = sem("max_ready")
        exp_done = sem("exp_done")
        norm_done = sem("norm_done")
        probT_ps, probT_sb = sem("probT_ps"), sem("probT_sb")
        pv_ps = sem("pv_ps")
        attn_out = sem("attn_out")
        stats_sb, gstats_ps = sem("stats_sb"), sem("gstats_ps")
        gvar_ready, grs_ready = sem("gvar_ready"), sem("grs_ready")
        h_ready = sem("h_ready")
        qkv1_ps, q1_sb, k1_sb, v1_sb = sem("qkv1_ps"), sem("q1_sb"), sem("k1_sb"), sem("v1_sb")
        kv2_border = sem("kv2_border")
        qkv2_ps, q2_sb, k2_sb, v2_sb = sem("qkv2_ps"), sem("q2_sb"), sem("k2_sb"), sem("v2_sb")
        prod_dve, prod_pool = sem("prod_dve"), sem("prod_pool")
        hexs_pair = sem("hexs_pair")
        hex_shift, hex_exp, att_ready = sem("hex_shift"), sem("hex_exp"), sem("att_ready")
        cast_ps, avprod_sb = sem("cast_ps"), sem("avprod_sb")
        av_used = sem("av_used")
        d_ps, sq_sb, var_ps, std_sb = sem("d_ps"), sem("sq_sb"), sem("var_ps"), sem("std_sb")
        xhat_sb, ln_out = sem("xhat_sb"), sem("ln_out")
        ff_ps, ff_sb = sem("ff_ps"), sem("ff_sb")
        c1_ps, c1_sb, c2_ps, c2_sb = sem("c1_ps"), sem("c1_sb"), sem("c2_ps"), sem("c2_sb")
        bn_ready, ctap_ready, cpad_ready = sem("bn_ready"), sem("ctap_ready"), sem("cpad_ready")
        c3_ps, x3_sb = sem("c3_ps"), sem("x3_sb")
        finT_ps, fin_sb = sem("finT_ps"), sem("fin_sb")

        def col(name, k=0):
            r = ROW[name] + k
            return vcol[:, r:r + 1]

        def hexview(buf, j, run, rows=SIDE, row0=0):
            (q0, r0), (q1_, r1_) = run[0], run[1]
            step = (r1_ - r0) * PAD + (q1_ - q0)
            base = buf[:, j, 1 + r0 + row0:1 + r0 + row0 + rows, 1 + q0:1 + q0 + SIDE]
            a = [list(x) for x in base.ap]
            return bass.AP(tensor=base.tensor, offset=base.offset,
                           ap=[a[0], [step, len(run)]] + a[1:])

        def rep(ap, n):
            a = [list(x) for x in ap.ap]
            return bass.AP(tensor=ap.tensor, offset=ap.offset, ap=[a[0], [0, n]] + a[1:])

        def dram_rep(ap, n):
            return bass.AP(tensor=ap.tensor, offset=ap.offset, ap=[[0, 1], [0, n], [1, ap.shape[0]]])

        EARLY, LATE, CONV = [], [], []
        for n, w in enumerate(("L0_conv_wq", "L0_conv_wk")):
            for i in range(2):
                EARLY.append((wqk0[64 * i:64 * i + 64, n, 32 * i:32 * i + RC], t[w]))
        for i in range(2):
            EARLY.append((wbd[64 * i:64 * i + 64, BD["L0_wv"], 64 * i:64 * i + 64], t["L0_conv_wv"]))
        for n in ("L0_conv_bq", "L0_conv_bk"):
            EARLY.append((vrows[ROW[n]:ROW[n] + 1, :].rearrange("a (n m) -> a n m", n=4)[:, :, 0:RC],
                          dram_rep(t[n], 4)))
        for n in VEC64:
            EARLY.append((vrows[ROW[n]:ROW[n] + 1, :].rearrange("a (n m) -> a n m", n=2), dram_rep(t[n], 2)))
        for n in VEC128:
            EARLY.append((vrows[ROW[n]:ROW[n] + 1, :], t[n].rearrange("(a m) -> a m", a=1)))
        for i in range(2):
            EARLY.append((vrows[ROW["in_proj_b"]:ROW["in_proj_b"] + 3, 64 * i:64 * i + 64],
                          t["L2_conv_in_proj_b"].rearrange("(a m) -> a m", a=3)))
        EARLY.append((vrows[ROW["L2_conv_b1"]:ROW["L2_conv_b1"] + FH, :],
                      t["L2_conv_b1"].rearrange("(a m) -> a m", a=FH)))
        for n, w in (("L1_Wq", "L1_conv_Wq"), ("L1_Wk", "L1_conv_Wk"), ("L1_Wv", "L1_conv_Wv"),
                     ("L1_Wo", "L1_conv_Wo"), ("out_w", "L2_conv_out_w")):
            for i in range(2):
                LATE.append((wbd[64 * i:64 * i + 64, BD[n], 64 * i:64 * i + 64], t[w]))
        for i in range(2):
            LATE.append((wbd[64 * i:64 * i + 64, BD["in_q"]:BD["in_q"] + 3, 64 * i:64 * i + 64],
                         t["L2_conv_in_proj_w"].rearrange("(a o) c -> o a c", a=3)))
            LATE.append((w1nat[:, :, i, :], t["L2_conv_w1"].rearrange("(h f) c -> f h c", h=FH)))
        LATE.append((w2nat[:, :], t["L2_conv_w2"]))
        for i in range(2):
            CONV.append((c1[64 * i:64 * i + 64, i, :], t["L3_conv_w1"][0, 0]))
        w2c_dram = t["L3_conv_w2"]
        for ci in range(4):
            CONV.append((craw[ci::4, :, :],
                         bass.AP(tensor=w2c_dram.tensor, offset=w2c_dram.offset + ci * CM,
                                 ap=[[0, 32], [4 * CM, 9], [1, CM]])))
        CONV.append((c3[:, :], t["L3_conv_w3"][0, 0]))
        VROW_DMAS = 2 + len(VEC64) + len(VEC128) + 3

        block = ctx.enter_context(nc.Block())

        NATT = 2 * IMAGES

        @block.sync
        def _(sp):
            for j in range(PAIRS):
                for i in (2 * j, 2 * j + 1):
                    sp.dma_start(xin[:, j, :, i % 2, :],
                                 t["x"][i].rearrange("h w c -> (h w) c")
                                          .rearrange("(p b) c -> p b c", b=BLK)).then_inc(x_in[j // 2], 16)
            sp.wait_ge(cleared, 3)
            for dst, src in EARLY[0::2]:
                sp.dma_start(dst, src).then_inc(w_early, 16)
            sp.wait_ge(cleared, 4)
            for dst, src in LATE:
                sp.dma_start(dst, src).then_inc(w_late, 16)
            for dst, src in CONV:
                sp.dma_start(dst, src).then_inc(w_conv, 16)
            for i in range(IMAGES):
                g, j, h = i // 4, (i // 2) % 2, i % 2
                sp.wait_ge(fin_sb, 2 * g + j + 1)
                sp.dma_start(out[i].rearrange("h w c -> (h w) c").rearrange("(p b) c -> p b c", b=BLK),
                             fin[:, i // 2, :, h, :]).then_inc(stored, 16)
            sp.wait_ge(stored, 16 * IMAGES)

        @block.gpsimd
        def _(pool):
            step = [0]

            def done(ins):
                step[0] += 1
                ins.then_inc(pool_step, 1)
                pool.wait_ge(pool_step, step[0])

            g = nc.gpsimd
            g.memset(ident[:, :], 0.0).then_inc(pool_step, 1)
            step[0] += 1
            pool.wait_ge(pool_step, step[0])
            g.affine_select(out=ident[:, :], in_=ident[:, :], compare_op=ALU.not_equal, fill=1.0,
                            base=0, pattern=[[-1, 128]], channel_multiplier=1).then_inc(id_ready, 1)
            for n in range(4):
                g.memset(k_mask[:, n:n + 1], 0.0).then_inc(pool_step, 1)
            step[0] += 4
            pool.wait_ge(pool_step, step[0])
            for n in range(4):
                done(g.memset(k_mask[32 * n:32 * n + 32, n:n + 1], 1.0))

            for n in range(IMAGES):
                if n % 4 == 0:
                    pool.wait_ge(qk0_sb, 2 * (n // 4 + 1))
                g.tensor_scalar(kz0[:, n, :], qk0[:, n // 4, 1, :], k_mask[:, n % 4:n % 4 + 1], None,
                                ALU.mult).then_inc(kz0_ready, 1)

            g.memset(mean64[:, :], 0.0).then_inc(pool_step, 1)
            g.memset(pairavg[:, :], 0.5).then_inc(pool_step, 1)
            g.memset(head_sum[:, :], 1.0).then_inc(pool_step, 1)
            g.memset(head_cast[:, :, :, :], 0.0).then_inc(pool_step, 1)
            g.memset(gmask[:, :], 1.0).then_inc(pool_step, 1)
            g.memset(minus_half[:, :], -0.5).then_inc(pool_step, 1)
            g.memset(epsln[:, :], EPS_LN).then_inc(pool_step, 1)
            step[0] += 7
            pool.wait_ge(pool_step, step[0])
            for i in range(2):
                done(g.memset(mean64[64 * i:64 * i + 64, 64 * i:64 * i + 64], 1.0 / CH))
            for low in (True, False):
                for m, size, n, inner, base in ((pairavg, 2, 64, 2, 0), (gmask, 4, 32, 4, 0),
                                                (head_sum, 8, 240, 1, -112)):
                    v = m[:, :].rearrange("p (a b) -> p a b", b=inner)
                    sign = 1 if low else -1
                    first = -size * base if low else size - 1 + size * base
                    g.affine_select(out=v, in_=v, compare_op=ALU.is_ge, fill=0.0,
                                    base=first, pattern=[[-sign * size, n], [0, inner]],
                                    channel_multiplier=sign).then_inc(pool_step, 1)
                step[0] += 3
                pool.wait_ge(pool_step, step[0])
            v = head_cast[:, :, :, :].rearrange("p s j (a b) -> p (s j) a b", b=HD)
            done(g.affine_select(out=v, in_=v, compare_op=ALU.not_equal, fill=1.0, base=0,
                                 pattern=[[-16, 2 * PAIRS], [-1, 16], [0, HD]], channel_multiplier=1))
            g.tensor_tensor(centre[:, :], ident[:, :], mean64[:, :], ALU.subtract).then_inc(consts, 1)

            pool.wait_ge(vcol_ready, 1)
            pool.wait_ge(cleared, 5)
            for buf, k in ((k2, 1), (v2, 2)):
                for h in range(GROUPS):
                    g.tensor_scalar(buf[:, 2 * h:2 * h + 2, :, :].rearrange("p a b c -> p (a b c)"),
                                    zeros[:, :], col("in_proj_b", k), None, ALU.add).then_inc(kv2_border, 1)

            pool.wait_ge(bn_ready, 1)
            g.tensor_tensor(bnr[:, :], bnv[:, :], minus_half[:, 0:2], ALU.pow).then_inc(bn_ready, 1)

            def group_rstd(gr):
                pool.wait_ge(gvar_ready, gr + 1)
                g.tensor_tensor(grs[:, 2 * gr:2 * gr + 2], gvar[:, 2 * gr:2 * gr + 2],
                                minus_half[:, 0:2], ALU.pow).then_inc(grs_ready, 1)

            group_rstd(0)
            pool.wait_ge(w_conv, 16 * len(CONV))
            g.tensor_tensor(ctap[:, :, :], craw[:, :, :], rep(gmask[:, :], 9), ALU.mult)\
                .then_inc(ctap_ready, 1)
            group_rstd(1)

            for j in range(PAIRS):
                pool.wait_ge(q2_sb, j // 2 + 1)
                pool.wait_ge(k2_sb, j // 2 + 1)
                if j >= 2:
                    pool.wait_ge(hexs_pair, j - 1)
                q = rep(q2[:, j, :].rearrange("p (a b) -> p a b", b=SIDE), 2)
                g.tensor_tensor(qkprod[:, j % 2, 5:7, :].rearrange("p k (a b) -> p k a b", b=SIDE),
                                q, hexview(k2, j, HEX_RUNS[2]), ALU.mult).then_inc(prod_pool, 1)

        @block.scalar
        def _(act):
            s = nc.scalar
            act.wait_ge(cleared, 3)
            for dst, src in EARLY[1::2]:
                act.dma_start(dst, src).then_inc(w_early, 16)

            def copy(dst, src):
                return s.activation(dst, src, ACT.Copy)

            act.wait_ge(vrow_ps, 1)
            copy(vcol[:, :], W_BANK[2][:, 0:ROWS]).then_inc(vcol_ready, 1)
            act.wait_ge(vcol_ready, 1)
            s.activation(qb8[:, :], col("L1_conv_bq"), ACT.Copy, scale=CH ** -0.5).then_inc(act_step, 1)

            def group0(gr):
                act.wait_ge(xT_ps, gr + 1)
                copy(xT[:, 2 * gr:2 * gr + 2, :], W_BANK[0][:, :]).then_inc(xT_sb, 1)
                act.wait_ge(qk0_ps, gr + 1)
                for n, b in enumerate(("L0_conv_bq", "L0_conv_bk")):
                    s.activation(qk0[:, gr, n, :], W_BANK[1][:, n * TOK:(n + 1) * TOK], ACT.Relu,
                                 bias=col(b)).then_inc(qk0_sb, 1)

            def exps(n):
                act.wait_ge(max_ready, n + 1)
                act.wait_ge(scores_ps, n + 1)
                if n >= 3:
                    act.wait_ge(norm_done, BLK * (n - 2))
                for b in range(BLK):
                    s.activation(prob[:, n % 3, b, :], S_BANK[n % 2][:, b * TOK:(b + 1) * TOK], ACT.Exp,
                                 bias=nmax[:, n, b:b + 1], accum_out=rsum[:, n, b:b + 1]).then_inc(exp_done, 1)

            def copy_probT(n):
                act.wait_ge(probT_ps, n + 1)
                if n >= 4:
                    act.wait_ge(pv_ps, n // 2 - 1)
                copy(probT[:, n % 4, :, :].rearrange("p a b -> p (a b)"), T_BANK[n % 2][:, :])\
                    .then_inc(probT_sb, 1)

            def group1(gr):
                act.wait_ge(act_step, 1)
                act.wait_ge(k1_sb, 2)
                act.wait_ge(qkv1_ps, 3 * gr + 1)
                s.activation(q1[:, 2 * gr:2 * gr + 2, :].rearrange("p a b -> p (a b)"), W_BANK[1],
                             ACT.Identity, bias=qb8[:, :], scale=CH ** -0.5).then_inc(q1_sb, 1)
                act.wait_ge(qkv1_ps, 3 * gr + 2)
                for i in range(2):
                    h = slice(64 * i, 64 * i + 64)
                    s.activation(kz1[h, 4 * gr + i:4 * gr + i + 3:2, :],
                                 W_BANK[2][h, :].rearrange("p (a b) -> p a b", a=2), ACT.Identity,
                                 bias=col("L1_conv_bk")[h]).then_inc(k1_sb, 1)

            def group2(gr):
                act.wait_ge(kv2_border, 4)
                act.wait_ge(qkv2_ps, 3 * gr + 1)
                s.activation(q2[:, 2 * gr:2 * gr + 2, :].rearrange("p a b -> p (a b)"), W_BANK[0],
                             ACT.Identity, bias=col("in_proj_b", 0)).then_inc(q2_sb, 1)
                act.wait_ge(qkv2_ps, 3 * gr + 2)
                for buf, n, k, done in ((k2, 1, 1, k2_sb),):
                    for j in range(2):
                        ins = s.activation(buf[:, 2 * gr + j, 1:1 + SIDE, 1:1 + SIDE],
                                           W_BANK[n][:, j * TOK:(j + 1) * TOK]
                                           .rearrange("p (a b) -> p a b", b=SIDE),
                                           ACT.Identity, bias=col("in_proj_b", k))
                    ins.then_inc(done, 1)

            group0(0)
            group0(1)
            for n in range(NATT + 2):
                if n < NATT:
                    exps(n)
                if 1 <= n <= NATT:
                    copy_probT(n - 1)
                if n == 6:
                    group1(0)
                if n == 10:
                    group1(1)
                if n == 14:
                    group2(0)
            group2(1)

            act.wait_ge(hex_shift, 1)
            s.activation(sexp[:, :, :].rearrange("p k n -> p (k n)"), sexp[:, :, :]
                         .rearrange("p k n -> p (k n)"), ACT.Exp, scale=float(HD) ** -0.5).then_inc(hex_exp, 1)

            def layer_norm(n, dst, gain, shift):
                gr = n % 2
                if n < 2:
                    act.wait_ge(av_used, 2 * n + 2)
                else:
                    act.wait_ge(d_ps, n - 1)
                act.wait_ge(prep_sb, 6)
                if n >= 2:
                    act.wait_ge(var_ps, n - 1)
                s.activation(sq[:, gr, :], duo[:, 512 * gr:512 * gr + 512], ACT.Square,
                             bias=cb[:, n // 2:n // 2 + 1]).then_inc(sq_sb, 1)
                act.wait_ge(var_ps, n + 1)
                if n >= 2:
                    act.wait_ge(xhat_sb, n - 1)
                s.activation(std[:, gr, :], bank[gr][:, :], ACT.Sqrt, bias=epsln[:, :]).then_inc(std_sb, 1)

            def ln_affine(n, dst, gain, shift):
                gr = n % 2
                act.wait_ge(xhat_sb, n + 1)
                s.activation(dst[:, gr, :], xhat[:, gr, :], ACT.Identity, bias=shift, scale=gain)\
                    .then_inc(ln_out, 1)

            for n in (0, 1):
                layer_norm(n, x1, None, None)
            for n in (0, 1):
                ln_affine(n, x1, col("L2_conv_g1"), col("L2_conv_beta1"))

            def relu_ff(m):
                gr, h, i = m // 4, (m // 2) % 2, m % 2
                act.wait_ge(ff_ps, m + 1)
                s.activation(ffh[:, gr, h, i, :], bank[2 + m % 4][:, :], ACT.Relu,
                             bias=col("L2_conv_b1", h)).then_inc(ff_sb, 1)

            for m in range(8):
                relu_ff(m)
            for n in (2, 3):
                layer_norm(n, x2, None, None)
            for n in (2, 3):
                ln_affine(n, x2, col("L2_conv_g2"), col("L2_conv_beta2"))
            act.wait_ge(bn_ready, 3)
            act.wait_ge(cpad_ready, 1)
            for m in range(4):
                act.wait_ge(c1_ps, m + 1)
                for j in range(2):
                    ins = s.activation(c1out[:, m // 2, m % 2, j, 1:1 + SIDE, 1:1 + SIDE],
                                       bank[2 + m][:, j * TOK:(j + 1) * TOK].rearrange("p (a b) -> p a b", b=SIDE),
                                       ACT.Relu, bias=bnsh[:, 0:1], scale=bninv[:, 0:1])
                ins.then_inc(c1_sb, 1)
            for m in range(4):
                act.wait_ge(c2_ps, m + 1)
                s.activation(c2out[:, m // 2, m % 2, :], bank[2 + m][:, :], ACT.Relu,
                             bias=bnsh[:, 1:2], scale=bninv[:, 1:2]).then_inc(c2_sb, 1)
            for gr in range(GROUPS):
                for j in range(2):
                    act.wait_ge(finT_ps, 2 * gr + j + 1)
                    s.activation(fin[:, 2 * gr + j, :, :, :].rearrange("p b i c -> p (b i c)"),
                                 bank[2 * gr + j][:, 0:256],
                                 ACT.Relu).then_inc(fin_sb, 1)

        @block.vector
        def _(dve):
            v = nc.vector
            step = [0]

            def done(ins):
                step[0] += 1
                ins.then_inc(dve_step, 1)
                dve.wait_ge(dve_step, step[0])

            v.memset(vrows[:, :], 0.0).then_inc(cleared, 1)
            v.memset(wqk0[:, :, :].rearrange("p a b -> p (a b)"), 0.0).then_inc(cleared, 1)
            v.memset(wbd[:, BD["L0_wv"], :], 0.0)
            v.memset(wbd[:, 1:, :].rearrange("p a b -> p (a b)"), 0.0).then_inc(cleared, 1)
            v.memset(c1[:, :, :].rearrange("p a b -> p (a b)"), 0.0).then_inc(cleared, 1)
            v.memset(zeros[:, :], 0.0).then_inc(cleared, 1)

            def values0(gr):
                dve.wait_ge(v0_ps, gr + 1)
                v.tensor_copy(v0[:, 4 * gr:4 * gr + 4, :].rearrange("p a b -> p (a b)"), W_BANK[2])\
                    .then_inc(v0_sb, 1)

            def maxes(n):
                dve.wait_ge(scores_ps, n + 1)
                v.tensor_reduce(nmax[:, n, :], S_BANK[n % 2][:, :].rearrange("p (b m) -> p b m", b=BLK),
                                AX.X, ALU.max, negate=True).then_inc(max_ready, 1)

            def normalise(n):
                dve.wait_ge(exp_done, BLK * (n + 1))
                done(v.reciprocal(rrec[:, n, :], rsum[:, n, :]))
                if n >= 2:
                    dve.wait_ge(probT_ps, n - 1)
                for b in range(BLK):
                    v.tensor_scalar(probn[:, n % 2, b, :], prob[:, n % 3, b, :], rrec[:, n, b:b + 1], None,
                                    ALU.mult).then_inc(norm_done, 1)

            def residual(p):
                j = p % PAIRS
                dve.wait_ge(pv_ps, p + 1)
                if p < PAIRS:
                    bias, src, dst = col("L0_conv_bv"), xT, yT
                else:
                    bias, src, dst = cb[:, 2:3], yT, zT
                if p == 0:
                    dve.wait_ge(vcol_ready, 1)
                o = dst[:, j, :] if p < PAIRS else dst[:, j, :].rearrange("p (n b) -> p b n", b=BLK)
                i = O_BANK[:, 0:TOK]
                r = src[:, j, :]
                if p >= PAIRS:
                    i, r = (x.rearrange("p (b n) -> p b n", b=BLK) for x in (i, r))
                v.scalar_tensor_tensor(out=o, in0=i, scalar=bias, in1=r, op0=ALU.add, op1=ALU.add)\
                    .then_inc(attn_out, 1)

            def stats(gr):
                dve.wait_ge(attn_out, 2 * gr + 2)
                for j in (2 * gr, 2 * gr + 1):
                    v.bn_stats(bnst[:, j, :], yT[:, j, :]).then_inc(dve_step, 1)
                step[0] += 2
                dve.wait_ge(dve_step, step[0])
                for j in (2 * gr, 2 * gr + 1):
                    v.bn_aggr(mv[:, j, :], bnst[:, j, :]).then_inc(dve_step, 1)
                step[0] += 2
                dve.wait_ge(dve_step, step[0])
                pr = slice(2 * gr, 2 * gr + 2)
                done(v.tensor_tensor(sq4[:, pr], mv[:, pr, 0], mv[:, pr, 0], ALU.mult))
                v.tensor_tensor(mv[:, pr, 1], mv[:, pr, 1], sq4[:, pr], ALU.add).then_inc(stats_sb, 1)

            def group_norm_a(gr):
                pr = slice(2 * gr, 2 * gr + 2)
                dve.wait_ge(gstats_ps, gr + 1)
                done(v.tensor_copy(gmv[:, pr, :].rearrange("p a b -> p (a b)"), W_BANK[0][:, 0:4]))
                done(v.tensor_tensor(gtmp[:, pr], gmv[:, pr, 0], gmv[:, pr, 0], ALU.mult))
                v.scalar_tensor_tensor(out=gvar[:, pr], in0=gmv[:, pr, 1], scalar=EPS_GN, in1=gtmp[:, pr],
                                       op0=ALU.add, op1=ALU.subtract).then_inc(gvar_ready, 1)

            def group_norm_b(gr):
                pr = slice(2 * gr, 2 * gr + 2)
                dve.wait_ge(grs_ready, gr + 1)
                done(v.tensor_scalar(gsc[:, pr], grs[:, pr], col("L1_conv_gn_scale"), None, ALU.mult))
                done(v.tensor_tensor(gtmp[:, pr], gmv[:, pr, 0], gsc[:, pr], ALU.mult))
                done(v.tensor_scalar(gbi[:, pr], gtmp[:, pr], -1.0, col("L1_conv_gn_bias"),
                                     ALU.mult, ALU.add))
                for j in (2 * gr, 2 * gr + 1):
                    v.tensor_scalar(hT[:, j, :], yT[:, j, :], gsc[:, j:j + 1], gbi[:, j:j + 1],
                                    ALU.mult, ALU.add).then_inc(h_ready, 1)

            def values1(gr):
                dve.wait_ge(qkv1_ps, 3 * gr + 3)
                v.tensor_copy(v1[:, 4 * gr:4 * gr + 4, :].rearrange("p a b -> p (a b)"), W_BANK[0])\
                    .then_inc(v1_sb, 1)

            def values2(gr):
                dve.wait_ge(kv2_border, 4)
                dve.wait_ge(qkv2_ps, 3 * gr + 3)
                for j in range(2):
                    ins = v.tensor_scalar(v2[:, 2 * gr + j, 1:1 + SIDE, 1:1 + SIDE],
                                          W_BANK[2][:, j * TOK:(j + 1) * TOK]
                                          .rearrange("p (a b) -> p a b", b=SIDE),
                                          col("in_proj_b", 2), None, ALU.add)
                ins.then_inc(v2_sb, 1)

            def prep_copy(k, dst, src):
                dve.wait_ge(prep_ps, k)
                return v.tensor_copy(dst, src)

            values0(0)
            values0(1)
            for n in range(NATT + 2):
                if n < NATT:
                    maxes(n)
                if 1 <= n <= NATT:
                    normalise(n - 1)
                if n == 1:
                    v.memset(kz1[:, 0:4, :].rearrange("p a b -> p (a b)"), 0.0).then_inc(k1_sb, 1)
                    prep_copy(1, wvT1[:, :], W_BANK[0][:, 0:128]).then_inc(prep_sb, 1)
                if n == 2:
                    v.memset(kz1[:, 4:8, :].rearrange("p a b -> p (a b)"), 0.0).then_inc(k1_sb, 1)
                    prep_copy(2, wvo1[:, :], W_BANK[1][:, 0:128]).then_inc(prep_sb, 1)
                if n == 3:
                    prep_copy(3, inT[:, :, :].rearrange("p a b -> p (a b)"), W_BANK[0][:, 0:384])\
                        .then_inc(prep_sb, 1)
                    for k, nm in enumerate(("L3_conv_v1", "L3_conv_v2")):
                        ins = v.tensor_scalar(bnv[:, k:k + 1], col(nm), EPS_BN, None, ALU.add)
                    ins.then_inc(bn_ready, 1)
                if n == 4:
                    prep_copy(4, outc[:, :], W_BANK[1][:, 0:128]).then_inc(prep_sb, 1)
                    v.memset(w1T[:, :, :, :].rearrange("p a b c -> p (a b c)"), 0.0).then_inc(dve_step, 1)
                    step[0] += 1
                    dve.wait_ge(dve_step, step[0])
                    dve.wait_ge(prep_ps, 5)
                    for i in range(2):
                        ins = v.tensor_copy(w1T[64 * i:64 * i + 64, i, :, :].rearrange("p a b -> p (a b)"),
                                            W_BANK[2][64 * i:64 * i + 64, 0:256])
                    ins.then_inc(prep_sb, 1)
                if n == 5:
                    dve.wait_ge(prep_ps, 6)
                    v.tensor_copy(w2c[:, :, :].rearrange("p a b -> p (a b)"), W_BANK[0][:, 0:128])
                    v.tensor_copy(cb[:, 0:2], W_BANK[0][:, 128:130])
                    v.scalar_tensor_tensor(out=cb[:, 2:3], in0=W_BANK[0][:, 130:131], scalar=0.0,
                                           in1=col("L1_conv_bo"), op0=ALU.add, op1=ALU.add)\
                        .then_inc(prep_sb, 1)
                if n == 12:
                    dve.wait_ge(bn_ready, 2)
                    for k, (gm, b, mn, be) in enumerate((("L3_conv_g1", "L3_conv_b1", "L3_conv_m1", "L3_conv_be1"),
                                                         ("L3_conv_g2", "L3_conv_b2", "L3_conv_m2", "L3_conv_be2"))):
                        done(v.tensor_tensor(bninv[:, k:k + 1], bnr[:, k:k + 1], col(gm), ALU.mult))
                        done(v.tensor_tensor(bnv[:, k:k + 1], col(b), col(mn), ALU.subtract))
                        ins = v.scalar_tensor_tensor(out=bnsh[:, k:k + 1], in0=bnv[:, k:k + 1],
                                                     scalar=bninv[:, k:k + 1], in1=col(be),
                                                     op0=ALU.mult, op1=ALU.add)
                    ins.then_inc(bn_ready, 1)
                if n >= 3 and n % 2 == 1:
                    residual((n - 3) // 2)
                if n == 5:
                    stats(0)
                if n == 6:
                    group_norm_a(0)
                    group_norm_b(0)
                    values1(0)
                if n == 9:
                    stats(1)
                if n == 10:
                    group_norm_a(1)
                    group_norm_b(1)
                    values1(1)
                if n == 14:
                    values2(0)
            values2(1)
            v.memset(c1out[:, :, :, :, :, :].rearrange("p a b c d e -> p (a b c d e)"), 0.0)\
                .then_inc(cpad_ready, 1)

            for j in range(PAIRS):
                dve.wait_ge(q2_sb, j // 2 + 1)
                dve.wait_ge(k2_sb, j // 2 + 1)
                if j >= 2:
                    dve.wait_ge(hexs_pair, j - 1)
                k0 = 0
                for run in HEX_RUNS[:2]:
                    q = rep(q2[:, j, :].rearrange("p (a b) -> p a b", b=SIDE), len(run))
                    ins = v.tensor_tensor(qkprod[:, j % 2, k0:k0 + len(run), :]
                                          .rearrange("p k (a b) -> p k a b", b=SIDE),
                                          q, hexview(k2, j, run), ALU.mult)
                    k0 += len(run)
                ins.then_inc(prod_dve, 1)
            dve.wait_ge(hexs_pair, PAIRS)
            sc = duo[:, 0:NB * 128]
            done(v.tensor_reduce(smax[:, :], sc.rearrange("p (k n) -> p n k", k=NB), AX.X, ALU.max))
            v.tensor_tensor(sexp[:, :, :], sc.rearrange("p (k n) -> p k n", k=NB), rep(smax[:, :], NB),
                            ALU.subtract).then_inc(hex_shift, 1)
            dve.wait_ge(hex_exp, 1)
            done(v.tensor_reduce(smax[:, :], sexp[:, :, :].rearrange("p k n -> p n k"), AX.X, ALU.add))
            done(v.reciprocal(smax[:, :], smax[:, :]))
            v.tensor_tensor(att[:, :, :], sexp[:, :, :], rep(smax[:, :], NB), ALU.mult).then_inc(att_ready, 1)
            for m in range(2 * PAIRS):
                j, h = m // 2, m % 2
                if j >= 2 and h == 0:
                    dve.wait_ge(av_used, j - 1)
                dve.wait_ge(cast_ps, m + 1)
                dve.wait_ge(v2_sb, j // 2 + 1)
                pair_banks = (bank[2 * (m % 2)], bank[2 * (m % 2) + 1])
                k0 = 0
                for r, run in enumerate(HEX_RUNS):
                    src, off = (pair_banks[0], 0) if r == 0 else (pair_banks[1], (k0 - 3) * 128)
                    ins = v.tensor_tensor(
                        avprod[:, j % 2, k0:k0 + len(run), 128 * h:128 * h + 128]
                        .rearrange("p k (a b) -> p k a b", b=SIDE),
                        src[:, off:off + 128 * len(run)].rearrange("p (k a b) -> p k a b", k=len(run), b=SIDE),
                        hexview(v2, j, run, SIDE // 2, SIDE // 2 * h), ALU.mult)
                    k0 += len(run)
                ins.then_inc(avprod_sb, 1)

            def layer_norm(n):
                gr = n % 2
                dve.wait_ge(std_sb, n + 1)
                done(v.reciprocal(rstd[:, gr, :], std[:, gr, :]))
                if n >= 2:
                    dve.wait_ge(ln_out, n - 1)
                v.scalar_tensor_tensor(out=xhat[:, gr, :], in0=duo[:, 512 * gr:512 * gr + 512],
                                       scalar=cb[:, n // 2:n // 2 + 1], in1=rstd[:, gr, :],
                                       op0=ALU.add, op1=ALU.mult).then_inc(xhat_sb, 1)

            for n in range(4):
                layer_norm(n)
            for gr in range(GROUPS):
                dve.wait_ge(c3_ps, gr + 1)
                dve.wait_ge(ln_out, 3 + gr)
                v.scalar_tensor_tensor(out=x3[:, gr, :], in0=duo[:, 512 * gr:512 * gr + 512],
                                       scalar=col("L3_conv_b3"), in1=x2[:, gr, :],
                                       op0=ALU.add, op1=ALU.add).then_inc(x3_sb, 1)

        @block.tensor
        def _(pe):
            mm = nc.tensor.matmul

            def w(name):
                return wbd[:, BD[name], :]

            pe.wait_ge(id_ready, 1)
            for gr in range(GROUPS):
                pe.wait_ge(x_in[gr], 16 * 4)
                if gr:
                    pe.wait_ge(xT_sb, gr)
                for j in range(2):
                    for b in range(BLK):
                        ins = nc.tensor.transpose(W_BANK[0][:, (2 * j + b) * 128:(2 * j + b + 1) * 128],
                                                  xin[:, 2 * gr + j, b, :, :].rearrange("p i c -> p (i c)"), ident[:, :])
                ins.then_inc(xT_ps, 1)
                if gr == 0:
                    pe.wait_ge(w_early, 16 * len(EARLY))
                    nc.tensor.transpose(W_BANK[2][:, 0:ROWS], vrows[:, :], ident[0:ROWS, 0:ROWS])\
                        .then_inc(vrow_ps, 1)
                    pe.wait_ge(vcol_ready, 1)
                pe.wait_ge(xT_sb, gr + 1)
                if gr:
                    pe.wait_ge(qk0_sb, 2 * gr)
                for j in range(2):
                    for n in range(2):
                        ins = mm(W_BANK[1][64 * j:64 * j + 64, n * TOK:(n + 1) * TOK], wqk0[:, n, :],
                                 xT[:, 2 * gr + j, :], start=True, stop=True)
                ins.then_inc(qk0_ps, 1)
                if gr:
                    pe.wait_ge(v0_sb, gr)
                for j in range(2):
                    for b in range(BLK):
                        ins = mm(W_BANK[2][:, (2 * j + b) * 128:(2 * j + b + 1) * 128],
                                 xT[:, 2 * gr + j, b * 128:b * 128 + 128], w("L0_wv"), start=True, stop=True)
                ins.then_inc(v0_ps, 1)

            def scores(n):
                if n >= 2:
                    pe.wait_ge(exp_done, BLK * (n - 1))
                if n < IMAGES:
                    pe.wait_ge(kz0_ready, n + 1)
                    q, k = qk0[:, n // 4, 0, :], kz0[:, n, :]
                else:
                    m = n - IMAGES
                    pe.wait_ge(q1_sb, m // 4 + 1)
                    pe.wait_ge(k1_sb, 2 * (m // 4 + 1) + 2)
                    q, k = q1[:, m // 2, :], kz1[:, m, :]
                for b in range(BLK):
                    ins = mm(S_BANK[n % 2][:, b * TOK:(b + 1) * TOK], q[:, b * 128:b * 128 + 128], k,
                             start=True, stop=True)
                ins.then_inc(scores_ps, 1)

            def transposes(n):
                pe.wait_ge(norm_done, BLK * (n + 1))
                if n >= 2:
                    pe.wait_ge(probT_sb, n - 1)
                for mb in range(BLK):
                    for b in range(BLK):
                        ins = nc.tensor.transpose(T_BANK[n % 2][:, mb * TOK + b * 128:mb * TOK + b * 128 + 128],
                                                  probn[:, n % 2, b, mb * 128:mb * 128 + 128], ident[:, :])
                ins.then_inc(probT_ps, 1)

            def attend(p):
                j = p % PAIRS
                pe.wait_ge(probT_sb, 2 * p + 2)
                if p:
                    pe.wait_ge(attn_out, p)
                if p < PAIRS:
                    pe.wait_ge(v0_sb, j // 2 + 1)
                    val = v0
                else:
                    pe.wait_ge(v1_sb, j // 2 + 1)
                    val = v1
                for mb in range(BLK):
                    for i in range(2):
                        ins = mm(O_BANK[64 * i:64 * i + 64, 0:TOK], val[:, 2 * j + mb, 64 * i:64 * i + 64],
                                 probT[:, (2 * p + i) % 4, mb, :], start=mb == 0, stop=mb == BLK - 1)
                ins.then_inc(pv_ps, 1)

            def prep(n):
                if n == 0:
                    pe.wait_ge(w_late, 16 * len(LATE))
                    pe.wait_ge(xT_sb, 2)
                    pe.wait_ge(qk0_sb, 4)
                    pe.wait_ge(v0_sb, 2)
                    nc.tensor.transpose(W_BANK[0][:, 0:128], w("L1_Wv"), ident[:, :]).then_inc(prep_ps, 1)
                if n == 1:
                    pe.wait_ge(prep_sb, 1)
                    mm(W_BANK[1][:, 0:128], wvT1[:, :], w("L1_Wo"), start=True, stop=True).then_inc(prep_ps, 1)
                if n == 2:
                    for k in range(3):
                        ins = nc.tensor.transpose(W_BANK[0][:, k * 128:k * 128 + 128],
                                                  wbd[:, BD["in_q"] + k, :], ident[:, :])
                    ins.then_inc(prep_ps, 1)
                if n == 3:
                    pe.wait_ge(prep_sb, 2)
                    pe.wait_ge(consts, 1)
                    mm(W_BANK[1][:, 0:128], w("out_w"), centre[:, :], start=True, stop=True).then_inc(prep_ps, 1)
                    for h in range(FH):
                        ins = nc.tensor.transpose(W_BANK[2][:, h * 128:h * 128 + 128],
                                                  w1nat[:, h, :, :].rearrange("p a b -> p (a b)"), ident[:, :])
                    ins.then_inc(prep_ps, 1)
                if n == 4:
                    pe.wait_ge(prep_sb, 3)
                    for h in range(FH):
                        mm(W_BANK[0][:, h * CH:h * CH + CH], w2nat[:, h * 128:h * 128 + 128],
                           centre[0:CH, 0:CH], start=True, stop=True)
                    for k, b in enumerate(("L2_conv_out_b", "L2_conv_b2")):
                        mm(W_BANK[0][:, 128 + k:129 + k], centre[:, :], col(b), start=True, stop=True)
                    mm(W_BANK[0][:, 130:131], w("L1_Wo"), col("L1_conv_bv"), start=True, stop=True)\
                        .then_inc(prep_ps, 1)

            def group_stats(gr):
                pe.wait_ge(stats_sb, gr + 1)
                pe.wait_ge(prep_sb, 6)
                if gr:
                    pe.wait_ge(v1_sb, gr)
                mm(W_BANK[0][:, 0:4], pairavg[:, :], mv[:, 2 * gr:2 * gr + 2, :].rearrange("p a b -> p (a b)"),
                   start=True, stop=True).then_inc(gstats_ps, 1)

            def project1(gr):
                pe.wait_ge(h_ready, 2 * gr + 2)
                h2 = hT[:, 2 * gr:2 * gr + 2, :].rearrange("p a b -> p (a b)")
                if gr:
                    pe.wait_ge(q1_sb, gr)
                mm(W_BANK[1], w("L1_Wq"), h2, start=True, stop=True).then_inc(qkv1_ps, 1)
                if gr:
                    pe.wait_ge(k1_sb, 2 * gr + 2)
                mm(W_BANK[2], w("L1_Wk"), h2, start=True, stop=True).then_inc(qkv1_ps, 1)
                for j in range(2):
                    for b in range(BLK):
                        ins = mm(W_BANK[0][:, (2 * j + b) * 128:(2 * j + b + 1) * 128],
                                 hT[:, 2 * gr + j, b * 128:b * 128 + 128], wvo1[:, :], start=True, stop=True)
                ins.then_inc(qkv1_ps, 1)

            def project2(gr):
                pe.wait_ge(attn_out, PAIRS + 2 * gr + 2)
                z = zT[:, 2 * gr:2 * gr + 2, :].rearrange("p a b -> p (a b)")
                if gr == 0:
                    pe.wait_ge(v1_sb, 2)
                    pe.wait_ge(q1_sb, 2)
                    pe.wait_ge(k1_sb, 6)
                for k, free in enumerate((q2_sb, k2_sb, v2_sb)):
                    if gr:
                        pe.wait_ge(free, gr)
                    mm(W_BANK[k], inT[:, k, :], z, start=True, stop=True).then_inc(qkv2_ps, 1)

            for n in range(NATT + 2):
                if n < NATT:
                    scores(n)
                prep(n)
                if n >= 1 and n <= NATT:
                    transposes(n - 1)
                if n >= 3 and n % 2 == 1:
                    attend((n - 3) // 2)
                if n == 6:
                    group_stats(0)
                    project1(0)
                if n == 10:
                    group_stats(1)
                    project1(1)
                if n == 14:
                    project2(0)
            project2(1)

            pe.wait_ge(q2_sb, 2)
            pe.wait_ge(k2_sb, 2)
            pe.wait_ge(v2_sb, 2)
            sc = duo[:, 0:NB * 128]
            for j in range(PAIRS):
                pe.wait_ge(prod_dve, j + 1)
                pe.wait_ge(prod_pool, j + 1)
                for h in range(2):
                    off = 112 - (64 * h + 16 * j)
                    first, last = j == 0 and h == 0, j == PAIRS - 1 and h == 1
                    for k0, k1 in ((0, 4), (4, NB)):
                        ins = mm(sc[:, k0 * 128:k1 * 128], head_sum[:, off:off + 128],
                                 qkprod[:, j % 2, k0:k1, 128 * h:128 * h + 128], start=first, stop=last)
                ins.then_inc(hexs_pair, 1)

            def cast(m):
                j, h = m // 2, m % 2
                if m == 0:
                    pe.wait_ge(att_ready, 1)
                    pe.wait_ge(probT_sb, NATT)
                    pe.wait_ge(exp_done, BLK * NATT)
                if m >= 2:
                    pe.wait_ge(avprod_sb, m - 1)
                for k0, k1, b in ((0, 3, bank[2 * (m % 2)]), (3, NB, bank[2 * (m % 2) + 1])):
                    ins = mm(b[:, 0:(k1 - k0) * 128], head_cast[:, h, j, :], att[:, k0:k1, :],
                             start=True, stop=True)
                ins.then_inc(cast_ps, 1)

            def out_proj(j):
                gr = j // 2
                o = duo[:, 512 * gr + TOK * (j % 2):512 * gr + TOK * (j % 2) + TOK]
                mm(o, centre[:, :], zT[:, j, :], start=True, stop=False)
                pe.wait_ge(avprod_sb, 2 * j + 2)
                for k in range(NB):
                    ins = mm(o, outc[:, :], avprod[:, j % 2, k, :], start=False, stop=k == NB - 1)
                ins.then_inc(av_used, 1)

            cast(0)
            cast(1)
            for j in range(PAIRS):
                if j + 1 < PAIRS:
                    cast(2 * j + 2)
                    cast(2 * j + 3)
                out_proj(j)

            def variance(n):
                pe.wait_ge(sq_sb, n + 1)
                if n == 0:
                    pe.wait_ge(avprod_sb, 2 * PAIRS)
                if n >= 2:
                    pe.wait_ge(std_sb, n - 1)
                mm(bank[n % 2][:, :], mean64[:, :], sq[:, n % 2, :], start=True, stop=True).then_inc(var_ps, 1)

            variance(0)
            variance(1)
            for m in range(8):
                gr, h, i = m // 4, (m // 2) % 2, m % 2
                pe.wait_ge(ln_out, gr + 1)
                if m >= 4:
                    pe.wait_ge(ff_sb, m - 3)
                mm(bank[2 + m % 4][:, :], w1T[:, i, h, :], x1[:, gr, :], start=True, stop=True).then_inc(ff_ps, 1)
            for gr in range(GROUPS):
                pe.wait_ge(xhat_sb, gr + 1)
                o = duo[:, 512 * gr:512 * gr + 512]
                mm(o, centre[:, :], x1[:, gr, :], start=True, stop=False)
                for h in range(FH):
                    pe.wait_ge(ff_sb, 4 * gr + 2 * h + 2)
                    for i in range(2):
                        ins = mm(o[64 * i:64 * i + 64, :], w2c[:, h, :], ffh[:, gr, h, i, :],
                                 start=False, stop=h == FH - 1)
                ins.then_inc(d_ps, 1)
            variance(2)
            variance(3)
            for m in range(4):
                gr, i = m // 2, m % 2
                if m == 0:
                    pe.wait_ge(w_conv, 16 * len(CONV))
                    pe.wait_ge(ff_sb, 8)
                pe.wait_ge(ln_out, 3 + gr)
                mm(bank[2 + m][:, :], c1[:, i, :], x2[:, gr, :], start=True, stop=True).then_inc(c1_ps, 1)
            for m in range(4):
                gr, i = m // 2, m % 2
                pe.wait_ge(c1_sb, m + 1)
                if m == 0:
                    pe.wait_ge(ctap_ready, 1)
                for tap in range(9):
                    ty, tx = tap // 3, tap % 3
                    ins = mm(bank[2 + m][:, :], ctap[:, tap, :],
                             c1out[:, gr, i, :, ty:ty + SIDE, tx:tx + SIDE], start=tap == 0, stop=tap == 8)
                ins.then_inc(c2_ps, 1)
            for gr in range(GROUPS):
                pe.wait_ge(xhat_sb, 3 + gr)
                for i in range(2):
                    pe.wait_ge(c2_sb, 2 * gr + i + 1)
                    ins = mm(duo[64 * i:64 * i + 64, 512 * gr:512 * gr + 512], c3[:, :], c2out[:, gr, i, :],
                             start=True, stop=True)
                ins.then_inc(c3_ps, 1)
            for gr in range(GROUPS):
                pe.wait_ge(x3_sb, gr + 1)
                pe.wait_ge(c2_sb, 4)
                pe.wait_ge(std_sb, 4)
                for j in range(2):
                    xv = x3[:, gr, j * TOK:(j + 1) * TOK].rearrange("p (n b) -> p b n", b=BLK)
                    for b in range(BLK):
                        ins = nc.tensor.transpose(bank[2 * gr + j][:, b * 128:b * 128 + 128], xv[:, b, :],
                                                  ident[:, :])
                    ins.then_inc(finT_ps, 1)


_OUT = "out_dram"


def kernel(**inputs):
    import numpy as np
    import concourse.bacc as bacc
    from concourse.bass_utils import run_bass_kernel_spmd

    nc = bacc.Bacc("TRN2", target_bir_lowering=False, num_devices=1)
    arrays, aps = {}, {}
    for name, a in inputs.items():
        a = np.ascontiguousarray(a)
        arrays[f"in_{name}"] = a
        aps[name] = nc.dram_tensor(f"in_{name}", a.shape, mybir.dt.from_np(a.dtype), kind="ExternalInput").ap()
    out = nc.dram_tensor(_OUT, (IMAGES, SIDE, SIDE, CH), F32, kind="ExternalOutput").ap()
    build(nc, aps, out)
    r = run_bass_kernel_spmd(nc, [arrays], core_ids=[0])
    return r.results[0][_OUT]
```

```python
from contextlib import ExitStack

import concourse.bass as bass
from concourse import mybir

F32 = mybir.dt.float32
F32R = mybir.dt.float32r
ALU = mybir.AluOpType
ACT = mybir.ActivationFunctionType
AX = mybir.AxisListType

IMAGES, SIDE, CH = 8, 16, 64
TOK = SIDE * SIDE
PAIRS = IMAGES // 2
GROUPS = PAIRS // 2
BLK = TOK // 128
RC = CH // 8
HEADS, HD = 8, 8
DFF = 256
FH = DFF // 128
CM = 128
PAD = SIDE + 2
HEX_RUNS = [[(-1, 0), (0, 0), (1, 0)], [(0, -1), (0, 1)], [(1, -1), (-1, 1)]]
NB = sum(len(run) for run in HEX_RUNS)
EPS_GN, EPS_LN, EPS_BN = 1e-6, 1e-5, 1e-3

VEC64 = ["L1_conv_gn_scale", "L1_conv_gn_bias", "L1_conv_bq", "L1_conv_bk", "L1_conv_bv",
         "L0_conv_bv", "L1_conv_bo", "L2_conv_out_b", "L2_conv_b2",
         "L2_conv_g1", "L2_conv_beta1", "L2_conv_g2", "L2_conv_beta2", "L3_conv_b3"]
VEC128 = ["L3_conv_b1", "L3_conv_g1", "L3_conv_be1", "L3_conv_m1", "L3_conv_v1",
          "L3_conv_b2", "L3_conv_g2", "L3_conv_be2", "L3_conv_m2", "L3_conv_v2"]
COL = {"L0_conv_bq": 0, "L0_conv_bk": 1}
for _name in VEC64 + VEC128:
    COL[_name] = len(COL)
COL["in_proj_b"] = len(COL)
COL["L2_conv_b1"] = len(COL) + 2
COLS = COL["L2_conv_b1"] + FH

STRIPS, CONV_BLOCKS = 4, CM // 32
PACKS = {
    "p0": [("wqk0", 128), ("wv0_bd", 128), ("vcol", COLS), ("ident", 128)],
    "p1": [("wq1_bd", 128), ("wk1_bd", 128), ("wv1T_bd", 128), ("wo1_bd", 128), ("pairavg", 128),
           ("centre", 128)],
    "p2": [("inT_bd", 3 * 128), ("outw_bd", 128), ("w1T", 2 * FH * 128), ("w2", DFF),
           ("mean64", 128), ("head_sum", 48), ("c1", 2 * CM), ("ctap", CONV_BLOCKS * 3 * 32), ("c3", CH)],
}


def pack_width(pack):
    return sum(n for _, n in PACKS[pack])


def build(nc, t, out):
    ctx = ExitStack()
    with ctx:
        def sb(name, *shape):
            return ctx.enter_context(nc.sbuf_tensor(name, list(shape), F32))

        def sem(name):
            return ctx.enter_context(nc.semaphore(name))

        low = [ctx.enter_context(nc.psum_tensor(f"bank{i}", [128, 512], F32)) for i in range(6)]
        duo = ctx.enter_context(nc.psum_tensor("duo", [128, 1024], F32))
        bank = [b[:, :] for b in low] + [duo[:, 0:512], duo[:, 512:1024]]
        S_BANK = bank[0:3]
        T_BANK = bank[3:5]
        O_BANK = bank[5]
        W_BANK = bank[6:8]
        CAST_BANKS = [(bank[0], bank[1]), (bank[2], bank[3])]
        D_BANK = bank[4:6]

        head_cast = sb("head_cast", 128, 2 * PAIRS, 128)
        head_cast_r = ctx.enter_context(nc.sbuf_tensor("head_cast_r", [128, 2 * PAIRS, 128], F32R))
        epsln = sb("epsln", 128, 1)
        minus_half = sb("minus_half", 128, 4)
        zeros = sb("zeros", 128, 2 * PAD * PAD)
        packed = {p: sb(p, 128, pack_width(p)) for p in PACKS}
        table = {}
        for p, parts in PACKS.items():
            at = 0
            for name, n in parts:
                table[name] = packed[p][:, at:at + n]
                at += n
        vcol, ident, centre = table["vcol"], table["ident"], table["centre"]
        inT = table["inT_bd"].rearrange("p (k m) -> p k m", k=3)
        w1T = table["w1T"].rearrange("p (i h m) -> p i h m", i=2, h=FH)
        head_sum = table["head_sum"]
        c1 = table["c1"].rearrange("p (i m) -> p i m", i=2)
        ctap = table["ctap"].rearrange("p (r t m) -> p r t m", r=CONV_BLOCKS, t=3)
        wvo1 = sb("wvo1", 128, 128)
        outc = sb("outc", 128, 128)
        w2c = sb("w2c", 128, FH, CH)
        cb = sb("cb", 128, 3)
        qb8 = sb("qb8", 128, 1)
        bnv = sb("bnv", 128, 2)
        bnr = sb("bnr", 128, 2)
        bninv = sb("bninv", 128, 2)
        bnsh = sb("bnsh", 128, 2)
        xT = sb("xT", 128, PAIRS, TOK)
        q0 = sb("q0", 128, GROUPS, TOK)
        kz0 = sb("kz0", 128, IMAGES, TOK)
        v0 = sb("v0", 128, PAIRS * BLK, 128)
        prob = sb("prob", 128, 3, BLK, TOK)
        probn = sb("probn", 128, 2, BLK, TOK)
        probT = sb("probT", 128, 4, BLK, TOK)
        nmax = sb("nmax", 128, 2 * IMAGES, BLK)
        rsum = sb("rsum", 128, 2 * IMAGES, BLK)
        rrec = sb("rrec", 128, 2 * IMAGES, BLK)
        yT = sb("yT", 128, PAIRS, TOK)
        bnst = sb("bnst", 128, PAIRS, 6)
        mv = sb("mv", 128, PAIRS, 2)
        sq4 = sb("sq4", 128, PAIRS)
        gmv = sb("gmv", 128, PAIRS, 2)
        gvar = sb("gvar", 128, PAIRS)
        grs = sb("grs", 128, PAIRS)
        gsc = sb("gsc", 128, PAIRS)
        gbi = sb("gbi", 128, PAIRS)
        gtmp = sb("gtmp", 128, PAIRS)
        hT = sb("hT", 128, PAIRS, TOK)
        q1 = sb("q1", 128, PAIRS, TOK)
        kz1 = sb("kz1", 128, IMAGES, TOK)
        v1 = sb("v1", 128, PAIRS * BLK, 128)
        zT = sb("zT", 128, PAIRS, TOK)
        q2 = sb("q2", 128, PAIRS, TOK)
        k2 = sb("k2", 128, PAIRS, PAD, PAD)
        v2 = sb("v2", 128, PAIRS, PAD, PAD)
        qkprod = sb("qkprod", 128, 2, NB, TOK)
        smax = sb("smax", 128, 128)
        sexp = sb("sexp", 128, NB, 128)
        att = sb("att", 128, NB, 128)
        att_hi = ctx.enter_context(nc.sbuf_tensor("att_hi", [128, NB, 128], F32R))
        att_lo = ctx.enter_context(nc.sbuf_tensor("att_lo", [128, NB, 128], F32R))
        avsum = sb("avsum", 128, 2, NB // 2, TOK)
        avprod = qkprod
        sq = sb("sq", 128, 2, 512)
        lnv = sb("lnv", 128, 2, 512)
        rstd = sb("rstd", 128, 2, 512)
        xhat = sb("xhat", 128, 2, 512)
        x1 = sb("x1", 128, GROUPS, 512)
        x2 = sb("x2", 128, GROUPS, 512)
        ffh = sb("ffh", 128, 2, FH, 2, 512)
        strips = sb("strips", 128, 2, CONV_BLOCKS, 2, PAD, SIDE)
        c2out = ffh[:, 0, :, :, :]
        x3 = sq
        fin = sb("fin", 128, GROUPS, 512)

        x_in = [sem(f"x_in{j}") for j in range(PAIRS)]
        tables_in = {p: sem(f"{p}_in") for p in PACKS}
        stored = sem("stored")
        zeroed = sem("zeroed")
        consts = sem("consts")
        pool_step = sem("pool_step")
        dve_step = sem("dve_step")
        qb8_ready = sem("qb8_ready")
        prep_ps = sem("prep_ps")
        prep_sb = sem("prep_sb")
        qk0_ps, q0_sb = sem("qk0_ps"), sem("q0_sb")
        kz0_act, kz0_dve = sem("kz0_act"), sem("kz0_dve")
        v0_ps, v0_sb = sem("v0_ps"), sem("v0_sb")
        scores_ps = sem("scores_ps")
        max_ready = sem("max_ready")
        exp_done = sem("exp_done")
        norm_done = sem("norm_done")
        probT_ps, probT_sb = sem("probT_ps"), sem("probT_sb")
        pv_ps = sem("pv_ps")
        attn_out = sem("attn_out")
        stats_sb, gstats_ps, gstats_sb = sem("stats_sb"), sem("gstats_ps"), sem("gstats_sb")
        gvar_ready, grs_ready = sem("gvar_ready"), sem("grs_ready")
        h_ready = sem("h_ready")
        qkv1_ps, q1_sb, k1_sb, v1_sb = sem("qkv1_ps"), sem("q1_sb"), sem("k1_sb"), sem("v1_sb")
        kv2_border = sem("kv2_border")
        qkv2_ps, q2_sb, k2_sb, v2_sb = sem("qkv2_ps"), sem("q2_sb"), sem("k2_sb"), sem("v2_sb")
        prod_dve, prod_pool = sem("prod_dve"), sem("prod_pool")
        hexs_ps, cast_r = sem("hexs_ps"), sem("cast_r")
        hex_shift, hex_exp, att_ready = sem("hex_shift"), sem("hex_exp"), sem("att_ready")
        cast_ps, avprod_sb, avsum_sb = sem("cast_ps"), sem("avprod_sb"), sem("avsum_sb")
        av_used = sem("av_used")
        d_ps, sq_sb, var_ps = sem("d_ps"), sem("sq_sb"), sem("var_ps")
        lnv_sb, rstd_sb = sem("lnv_sb"), sem("rstd_sb")
        xhat_sb, ln_out = sem("xhat_sb"), sem("ln_out")
        ff_ps, ff_act, ff_dve = sem("ff_ps"), sem("ff_act"), sem("ff_dve")
        c1_ps, c1_sb, c2_ps, c2_sb = sem("c1_ps"), sem("c1_sb"), sem("c2_ps"), sem("c2_sb")
        shift_dve, shift_pool = sem("shift_dve"), sem("shift_pool")
        bn_ready = sem("bn_ready")
        c3_ps, fin_sb = sem("c3_ps"), sem("fin_sb")

        def col(name, k=0):
            r = COL[name] + k
            return vcol[:, r:r + 1]

        def hexview(buf, j, run, rows=SIDE, row0=0):
            (q0, r0), (q1_, r1_) = run[0], run[1]
            step = (r1_ - r0) * PAD + (q1_ - q0)
            base = buf[:, j, 1 + r0 + row0:1 + r0 + row0 + rows, 1 + q0:1 + q0 + SIDE]
            a = [list(x) for x in base.ap]
            return bass.AP(tensor=base.tensor, offset=base.offset,
                           ap=[a[0], [step, len(run)]] + a[1:])

        def rep(ap, n):
            a = [list(x) for x in ap.ap]
            return bass.AP(tensor=ap.tensor, offset=ap.offset, ap=[a[0], [0, n]] + a[1:])

        block = ctx.enter_context(nc.Block())

        NATT = 2 * IMAGES
        SLOTS = NATT + 4
        L0_BANKS = [(bank[6], bank[7], bank[5]), (bank[3], bank[4], bank[2])]

        def flat(ap):
            return ap.rearrange("p a b -> p (a b)")

        def shift(engine, c, r, s):
            d, f = (slice(1, SIDE), slice(0, SIDE - 1)) if s == 0 else (slice(0, SIDE - 1), slice(1, SIDE))
            return engine.tensor_copy(strips[32 * s:32 * s + 32, c % 2, r, :, 1:1 + SIDE, d],
                                      strips[32:64, c % 2, r, :, 1:1 + SIDE, f])

        @block.sync
        def _(sp):
            xd = t["xT"].rearrange("p (j n) -> p j n", j=PAIRS)
            for j in (0, 1):
                sp.dma_start(xT[:, j, :], xd[:, j, :]).then_inc(x_in[j], 16)
            for j in (2, 3):
                sp.dma_start(xT[:, j, :], xd[:, j, :]).then_inc(x_in[j], 16)
            sp.dma_start(packed["p2"][:, :], t["p2"]).then_inc(tables_in["p2"], 16)
            for gr in range(GROUPS):
                sp.wait_ge(fin_sb, gr + 1)
                sp.dma_start(out[:, 512 * gr:512 * gr + 512], fin[:, gr, :]).then_inc(stored, 16)
            sp.wait_ge(stored, 16 * GROUPS)

        @block.gpsimd
        def _(pool):
            g = nc.gpsimd
            g.memset(flat(kz0[:, :, :]), 0.0).then_inc(zeroed, 1)
            g.memset(flat(kz1[:, :, :]), 0.0).then_inc(zeroed, 1)
            g.memset(strips[:, :, :, :, :, :].rearrange("p a b c d e -> p (a b c d e)"), 0.0)\
                .then_inc(zeroed, 1)
            g.memset(flat(head_cast[:, :, :]), 0.0).then_inc(pool_step, 1)
            g.memset(minus_half[:, :], -0.5).then_inc(pool_step, 1)
            g.memset(epsln[:, :], EPS_LN).then_inc(pool_step, 1)
            g.memset(zeros[:, :], 0.0).then_inc(pool_step, 1)
            pool.wait_ge(pool_step, 4)
            v = head_cast[:, :, :].rearrange("p u (a b) -> p u a b", b=HD)
            g.affine_select(out=v, in_=v, compare_op=ALU.not_equal, fill=1.0, base=0,
                            pattern=[[-16, 2 * PAIRS], [-1, 16], [0, HD]], channel_multiplier=1)\
                .then_inc(consts, 1)

            pool.wait_ge(tables_in["p0"], 16)
            for buf, k in ((k2, 1), (v2, 2)):
                for h in range(GROUPS):
                    g.tensor_scalar(buf[:, 2 * h:2 * h + 2, :, :].rearrange("p a b c -> p (a b c)"),
                                    zeros[:, :], col("in_proj_b", k), None, ALU.add).then_inc(kv2_border, 1)

            pool.wait_ge(bn_ready, 1)
            g.tensor_tensor(bnr[:, :], bnv[:, :], minus_half[:, 0:2], ALU.pow).then_inc(bn_ready, 1)

            for gr in range(GROUPS):
                pool.wait_ge(gvar_ready, gr + 1)
                g.tensor_tensor(grs[:, 2 * gr:2 * gr + 2], gvar[:, 2 * gr:2 * gr + 2],
                                minus_half[:, 0:2], ALU.pow).then_inc(grs_ready, 1)

            for j in range(PAIRS):
                pool.wait_ge(q2_sb, j // 2 + 1)
                pool.wait_ge(k2_sb, j // 2 + 1)
                if j == 2:
                    pool.wait_ge(hexs_ps, 1)
                q = rep(q2[:, j, :].rearrange("p (a b) -> p a b", b=SIDE), 2)
                g.tensor_tensor(qkprod[:, j % 2, 5:7, :].rearrange("p k (a b) -> p k a b", b=SIDE),
                                q, hexview(k2, j, HEX_RUNS[2]), ALU.mult).then_inc(prod_pool, 1)
            for j in range(PAIRS):
                pool.wait_ge(avprod_sb, 2 * j + 2)
                if j >= 2:
                    pool.wait_ge(av_used, j - 1)
                g.tensor_tensor(avsum[:, j % 2, :, :], avprod[:, j % 2, 0:NB - 1:2, :],
                                avprod[:, j % 2, 1:NB - 1:2, :], ALU.add).then_inc(avsum_sb, 1)
            for c in range(4):
                pool.wait_ge(c1_sb, CONV_BLOCKS * (c + 1))
                shift(g, c, 3, 0)
                shift(g, c, 3, 2).then_inc(shift_pool, 1)

        @block.scalar
        def _(act):
            s = nc.scalar
            for p in ("p0", "p1"):
                act.dma_start(packed[p][:, :], t[p]).then_inc(tables_in[p], 16)
            act.wait_ge(tables_in["p0"], 16)
            s.activation(qb8[:, :], col("L1_conv_bq"), ACT.Copy, scale=CH ** -0.5).then_inc(qb8_ready, 1)
            act.wait_ge(zeroed, 1)
            for gr in range(GROUPS):
                act.wait_ge(qk0_ps, gr + 1)
                qb, kb, _ = L0_BANKS[gr]
                s.activation(q0[:, gr, :], qb[:, 0:TOK], ACT.Relu, bias=col("L0_conv_bq")).then_inc(q0_sb, 1)
                for n in range(2):
                    h = slice(32 * n, 32 * n + 32)
                    s.activation(kz0[h, 4 * gr + n, :], kb[h, 0:TOK], ACT.Relu,
                                 bias=col("L0_conv_bk")[h]).then_inc(kz0_act, 1)

            def exps(n):
                act.wait_ge(max_ready, n + 1)
                if n >= 3:
                    act.wait_ge(norm_done, BLK * (n - 2))
                for b in range(BLK):
                    s.activation(prob[:, n % 3, b, :], S_BANK[n % 3][:, b * TOK:(b + 1) * TOK], ACT.Exp,
                                 bias=nmax[:, n, b:b + 1], accum_out=rsum[:, n, b:b + 1]).then_inc(exp_done, 1)

            def copy_probT(n):
                act.wait_ge(probT_ps, n + 1)
                if n >= 4:
                    act.wait_ge(pv_ps, n // 2 - 1)
                s.activation(flat(probT[:, n % 4, :, :]), T_BANK[n % 2], ACT.Copy).then_inc(probT_sb, 1)

            def keys_queries1(gr):
                if gr == 0:
                    act.wait_ge(qb8_ready, 1)
                    act.wait_ge(zeroed, 2)
                act.wait_ge(qkv1_ps, 3 * gr + 1)
                s.activation(flat(q1[:, 2 * gr:2 * gr + 2, :]), W_BANK[0],
                             ACT.Identity, bias=qb8[:, :], scale=CH ** -0.5).then_inc(q1_sb, 1)
                act.wait_ge(qkv1_ps, 3 * gr + 2)
                for i in range(2):
                    h = slice(64 * i, 64 * i + 64)
                    s.activation(kz1[h, 4 * gr + i:4 * gr + i + 3:2, :],
                                 W_BANK[1][h, :].rearrange("p (a b) -> p a b", a=2), ACT.Identity,
                                 bias=col("L1_conv_bk")[h]).then_inc(k1_sb, 1)

            def keys_queries2(gr, banks):
                act.wait_ge(kv2_border, 4)
                act.wait_ge(qkv2_ps, 3 * gr + 1)
                s.activation(flat(q2[:, 2 * gr:2 * gr + 2, :]), banks[0],
                             ACT.Identity, bias=col("in_proj_b", 0)).then_inc(q2_sb, 1)
                act.wait_ge(qkv2_ps, 3 * gr + 2)
                s.activation(k2[:, 2 * gr:2 * gr + 2, 1:1 + SIDE, 1:1 + SIDE],
                             banks[1].rearrange("p (j a b) -> p j a b", j=2, b=SIDE),
                             ACT.Identity, bias=col("in_proj_b", 1)).then_inc(k2_sb, 1)

            for n in range(SLOTS):
                if n < NATT:
                    exps(n)
                if 2 <= n < NATT + 2:
                    copy_probT(n - 2)
                if n in (7, 11):
                    keys_queries1(n // 4 - 1)
                if n == 15:
                    keys_queries2(0, W_BANK)
            keys_queries2(1, S_BANK)

            act.wait_ge(hex_shift, 1)
            s.activation(flat(sexp[:, :, :]), flat(sexp[:, :, :]), ACT.Exp, scale=float(HD) ** -0.5)\
                .then_inc(hex_exp, 1)

            def squares(n):
                if n < 2:
                    act.wait_ge(av_used, 2 * n + 2)
                else:
                    act.wait_ge(d_ps, n - 1)
                    act.wait_ge(var_ps, n - 1)
                s.activation(sq[:, n % 2, :], D_BANK[n % 2], ACT.Square, bias=cb[:, n // 2:n // 2 + 1])\
                    .then_inc(sq_sb, 1)

            def inverse_std(n):
                act.wait_ge(var_ps, n + 1)
                s.activation(lnv[:, n % 2, :], bank[6], ACT.Ln, bias=epsln[:, :]).then_inc(lnv_sb, 1)
                act.wait_ge(lnv_sb, n + 1)
                if n >= 2:
                    act.wait_ge(xhat_sb, n - 1)
                s.activation(rstd[:, n % 2, :], lnv[:, n % 2, :], ACT.Exp, scale=-0.5).then_inc(rstd_sb, 1)

            def relu_ff(gr):
                for h in range(FH):
                    m = 4 * gr + 2 * h
                    act.wait_ge(ff_ps, m + 1)
                    s.activation(ffh[:, gr, h, 0, :], bank[m % 4], ACT.Relu,
                                 bias=col("L2_conv_b1", h)).then_inc(ff_act, 1)

            def conv1_out(c):
                act.wait_ge(c1_ps, c + 1)
                if c == 0:
                    act.wait_ge(bn_ready, 3)
                    act.wait_ge(zeroed, 3)
                if c >= 2:
                    act.wait_ge(c2_ps, c - 1)
                for r in range(CONV_BLOCKS):
                    h = slice(32 * r, 32 * r + 32)
                    s.activation(strips[32:64, c % 2, r, :, 1:1 + SIDE, :],
                                 bank[c][h, :].rearrange("p (j a b) -> p j a b", j=2, b=SIDE),
                                 ACT.Relu, bias=bnsh[h, 0:1], scale=bninv[h, 0:1]).then_inc(c1_sb, 1)

            def conv2_out(c):
                act.wait_ge(c2_ps, c + 1)
                s.activation(c2out[:, c // 2, c % 2, :], bank[7 - c % 2], ACT.Relu,
                             bias=bnsh[:, 1:2], scale=bninv[:, 1:2]).then_inc(c2_sb, 1)

            squares(0)
            inverse_std(0)
            squares(1)
            relu_ff(0)
            inverse_std(1)
            squares(2)
            relu_ff(1)
            inverse_std(2)
            squares(3)
            conv1_out(0)
            inverse_std(3)
            conv1_out(1)
            conv2_out(0)
            conv1_out(2)
            conv2_out(1)
            conv1_out(3)
            conv2_out(2)
            conv2_out(3)

        @block.vector
        def _(dve):
            v = nc.vector
            step = [0]

            def done(ins):
                step[0] += 1
                ins.then_inc(dve_step, 1)
                dve.wait_ge(dve_step, step[0])

            dve.wait_ge(tables_in["p0"], 16)
            dve.wait_ge(zeroed, 1)
            for gr in range(GROUPS):
                dve.wait_ge(qk0_ps, gr + 1)
                for n in range(2, 4):
                    h = slice(32 * n, 32 * n + 32)
                    v.tensor_scalar(kz0[h, 4 * gr + n, :], L0_BANKS[gr][1][h, 0:TOK],
                                    col("L0_conv_bk")[h], 0.0, ALU.add, ALU.max).then_inc(kz0_dve, 1)
                dve.wait_ge(v0_ps, gr + 1)
                v.tensor_copy(flat(v0[:, 4 * gr:4 * gr + 4, :]), L0_BANKS[gr][2]).then_inc(v0_sb, 1)

            def maxes(n):
                dve.wait_ge(scores_ps, n + 1)
                v.tensor_reduce(nmax[:, n, :], S_BANK[n % 3].rearrange("p (b m) -> p b m", b=BLK),
                                AX.X, ALU.max, negate=True).then_inc(max_ready, 1)

            def normalise(n):
                dve.wait_ge(exp_done, BLK * (n + 1))
                done(v.reciprocal(rrec[:, n, :], rsum[:, n, :]))
                if n >= 2:
                    dve.wait_ge(probT_ps, n - 1)
                for b in range(BLK):
                    v.tensor_scalar(probn[:, n % 2, b, :], prob[:, n % 3, b, :], rrec[:, n, b:b + 1], None,
                                    ALU.mult).then_inc(norm_done, 1)

            def residual(p):
                j = p % PAIRS
                dve.wait_ge(pv_ps, p + 1)
                bias, src, dst = (col("L0_conv_bv"), xT, yT) if p < PAIRS else (cb[:, 2:3], yT, zT)
                v.scalar_tensor_tensor(out=dst[:, j, :], in0=O_BANK[:, 0:TOK], scalar=bias, in1=src[:, j, :],
                                       op0=ALU.add, op1=ALU.add).then_inc(attn_out, 1)

            def stats(gr):
                dve.wait_ge(attn_out, 2 * gr + 2)
                pr = slice(2 * gr, 2 * gr + 2)
                for f, o, i in ((v.bn_stats, bnst, yT), (v.bn_aggr, mv, bnst)):
                    for j in (2 * gr, 2 * gr + 1):
                        f(o[:, j, :], i[:, j, :]).then_inc(dve_step, 1)
                    step[0] += 2
                    dve.wait_ge(dve_step, step[0])
                done(v.tensor_tensor(sq4[:, pr], mv[:, pr, 0], mv[:, pr, 0], ALU.mult))
                v.tensor_tensor(mv[:, pr, 1], mv[:, pr, 1], sq4[:, pr], ALU.add).then_inc(stats_sb, 1)

            def group_variance(gr):
                pr = slice(2 * gr, 2 * gr + 2)
                dve.wait_ge(gstats_ps, gr + 1)
                v.tensor_copy(flat(gmv[:, pr, :]), W_BANK[0][:, 0:4]).then_inc(gstats_sb, 1)
                dve.wait_ge(gstats_sb, gr + 1)
                done(v.tensor_tensor(gtmp[:, pr], gmv[:, pr, 0], gmv[:, pr, 0], ALU.mult))
                v.scalar_tensor_tensor(out=gvar[:, pr], in0=gmv[:, pr, 1], scalar=EPS_GN, in1=gtmp[:, pr],
                                       op0=ALU.add, op1=ALU.subtract).then_inc(gvar_ready, 1)

            def group_norm(gr):
                pr = slice(2 * gr, 2 * gr + 2)
                dve.wait_ge(grs_ready, gr + 1)
                done(v.tensor_scalar(gsc[:, pr], grs[:, pr], col("L1_conv_gn_scale"), None, ALU.mult))
                done(v.tensor_tensor(gtmp[:, pr], gmv[:, pr, 0], gsc[:, pr], ALU.mult))
                done(v.tensor_scalar(gbi[:, pr], gtmp[:, pr], -1.0, col("L1_conv_gn_bias"),
                                     ALU.mult, ALU.add))
                for j in (2 * gr, 2 * gr + 1):
                    v.tensor_scalar(hT[:, j, :], yT[:, j, :], gsc[:, j:j + 1], gbi[:, j:j + 1],
                                    ALU.mult, ALU.add).then_inc(h_ready, 1)

            def values1(gr):
                dve.wait_ge(qkv1_ps, 3 * gr + 3)
                v.tensor_copy(flat(v1[:, 4 * gr:4 * gr + 4, :]), W_BANK[0]).then_inc(v1_sb, 1)

            def values2(gr, b):
                dve.wait_ge(kv2_border, 4)
                dve.wait_ge(qkv2_ps, 3 * gr + 3)
                v.tensor_scalar(v2[:, 2 * gr:2 * gr + 2, 1:1 + SIDE, 1:1 + SIDE],
                                b.rearrange("p (j a b) -> p j a b", j=2, b=SIDE),
                                col("in_proj_b", 2), None, ALU.add).then_inc(v2_sb, 1)

            def prepared():
                dve.wait_ge(prep_ps, 1)
                v.tensor_copy(wvo1[:, :], W_BANK[0][:, 0:128])
                v.tensor_copy(outc[:, :], W_BANK[0][:, 128:256])
                v.tensor_copy(flat(w2c[:, :, :]), W_BANK[0][:, 256:384])
                v.tensor_copy(cb[:, 0:2], W_BANK[0][:, 384:386])
                v.tensor_tensor(cb[:, 2:3], W_BANK[0][:, 386:387], col("L1_conv_bo"), ALU.add)\
                    .then_inc(prep_sb, 1)

            def batch_norm_variances():
                for k, nm in enumerate(("L3_conv_v1", "L3_conv_v2")):
                    ins = v.tensor_scalar(bnv[:, k:k + 1], col(nm), EPS_BN, None, ALU.add)
                ins.then_inc(bn_ready, 1)

            def batch_norm():
                dve.wait_ge(bn_ready, 2)
                for k, (gm, b, mn, be) in enumerate((("L3_conv_g1", "L3_conv_b1", "L3_conv_m1", "L3_conv_be1"),
                                                     ("L3_conv_g2", "L3_conv_b2", "L3_conv_m2", "L3_conv_be2"))):
                    v.tensor_tensor(bnv[:, k:k + 1], col(b), col(mn), ALU.subtract)
                    done(v.tensor_tensor(bninv[:, k:k + 1], bnr[:, k:k + 1], col(gm), ALU.mult))
                    ins = v.scalar_tensor_tensor(out=bnsh[:, k:k + 1], in0=bnv[:, k:k + 1],
                                                 scalar=bninv[:, k:k + 1], in1=col(be),
                                                 op0=ALU.mult, op1=ALU.add)
                ins.then_inc(bn_ready, 1)

            def key_products(gr):
                for j in (2 * gr, 2 * gr + 1):
                    dve.wait_ge(q2_sb, gr + 1)
                    dve.wait_ge(k2_sb, gr + 1)
                    if gr:
                        dve.wait_ge(hexs_ps, gr)
                    k0 = 0
                    for run in HEX_RUNS[:2]:
                        q = rep(q2[:, j, :].rearrange("p (a b) -> p a b", b=SIDE), len(run))
                        ins = v.tensor_tensor(qkprod[:, j % 2, k0:k0 + len(run), :]
                                              .rearrange("p k (a b) -> p k a b", b=SIDE),
                                              q, hexview(k2, j, run), ALU.mult)
                        k0 += len(run)
                    ins.then_inc(prod_dve, 1)

            for n in range(SLOTS):
                if n < NATT:
                    maxes(n)
                if n in (7, 11):
                    group_variance(n // 4 - 1)
                if n in (8, 12):
                    values1(n // 4 - 2)
                if n >= 4 and n % 2 == 0:
                    residual((n - 4) // 2)
                if n in (6, 10):
                    stats((n - 6) // 4)
                if 1 <= n <= NATT:
                    normalise(n - 1)
                if n in (7, 11):
                    group_norm(n // 4 - 1)
                if n == 3:
                    batch_norm_variances()
                if n == 4:
                    prepared()
                if n == 9:
                    v.tensor_copy(flat(head_cast_r[:, :, :]), flat(head_cast[:, :, :])).then_inc(cast_r, 1)
                if n == 13:
                    batch_norm()
                if n == 16:
                    values2(0, W_BANK[0])
                    key_products(0)
            values2(1, S_BANK[2])
            key_products(1)

            dve.wait_ge(hexs_ps, GROUPS)
            sc = duo[:, 0:NB * 128]
            done(v.tensor_reduce(smax[:, :], sc.rearrange("p (k n) -> p n k", k=NB), AX.X, ALU.max))
            v.tensor_tensor(sexp[:, :, :], sc.rearrange("p (k n) -> p k n", k=NB), rep(smax[:, :], NB),
                            ALU.subtract).then_inc(hex_shift, 1)
            dve.wait_ge(hex_exp, 1)
            done(v.tensor_reduce(smax[:, :], sexp[:, :, :].rearrange("p k n -> p n k"), AX.X, ALU.add))
            done(v.reciprocal(smax[:, :], smax[:, :]))
            for k0, k1 in ((0, 3), (3, NB)):
                done(v.tensor_tensor(att[:, k0:k1, :], sexp[:, k0:k1, :], rep(smax[:, :], k1 - k0), ALU.mult))
                done(v.tensor_copy(att_hi[:, k0:k1, :], att[:, k0:k1, :]))
                v.tensor_tensor(att_lo[:, k0:k1, :], att[:, k0:k1, :], att_hi[:, k0:k1, :].bitcast(F32),
                                ALU.subtract).then_inc(att_ready, 1)

            for m in range(2 * PAIRS):
                j, h = m // 2, m % 2
                if j >= 2 and h == 0:
                    dve.wait_ge(av_used, j - 1)
                    dve.wait_ge(avsum_sb, j - 1)
                dve.wait_ge(cast_ps, m + 1)
                k0 = 0
                for n, run in enumerate(HEX_RUNS):
                    src, off = (CAST_BANKS[m % 2][0], 0) if n == 0 else (CAST_BANKS[m % 2][1], (k0 - 3) * 128)
                    ins = v.tensor_tensor(
                        avprod[:, j % 2, k0:k0 + len(run), 128 * h:128 * h + 128]
                        .rearrange("p k (a b) -> p k a b", b=SIDE),
                        src[:, off:off + 128 * len(run)].rearrange("p (k a b) -> p k a b", k=len(run), b=SIDE),
                        hexview(v2, j, run, SIDE // 2, SIDE // 2 * h), ALU.mult)
                    k0 += len(run)
                ins.then_inc(avprod_sb, 1)

            def layer_norm(n):
                gr = n % 2
                dst, gain, shift = ((x1, "L2_conv_g1", "L2_conv_beta1") if n < 2
                                    else (x2, "L2_conv_g2", "L2_conv_beta2"))
                dve.wait_ge(rstd_sb, n + 1)
                v.scalar_tensor_tensor(out=xhat[:, gr, :], in0=D_BANK[gr], scalar=cb[:, n // 2:n // 2 + 1],
                                       in1=rstd[:, gr, :], op0=ALU.add, op1=ALU.mult).then_inc(xhat_sb, 1)
                dve.wait_ge(xhat_sb, n + 1)
                v.tensor_scalar(dst[:, gr, :], xhat[:, gr, :], col(gain), col(shift), ALU.mult, ALU.add)\
                    .then_inc(ln_out, 1)

            def relu_ff(gr):
                for h in range(FH):
                    m = 4 * gr + 2 * h + 1
                    dve.wait_ge(ff_ps, m + 1)
                    v.tensor_scalar(ffh[:, gr, h, 1, :], bank[m % 4], col("L2_conv_b1", h), 0.0,
                                    ALU.add, ALU.max).then_inc(ff_dve, 1)

            def shifts(c):
                if c >= 2:
                    dve.wait_ge(c2_ps, c - 1)
                for r in range(CONV_BLOCKS - 1):
                    dve.wait_ge(c1_sb, CONV_BLOCKS * c + r + 1)
                    shift(v, c, r, 0)
                    shift(v, c, r, 2).then_inc(shift_dve, 1)

            def finish(gr):
                dve.wait_ge(c3_ps, gr + 1)
                done(v.scalar_tensor_tensor(out=x3[:, gr, :], in0=D_BANK[gr], scalar=col("L3_conv_b3"),
                                            in1=x2[:, gr, :], op0=ALU.add, op1=ALU.add))
                v.tensor_scalar(fin[:, gr, :], x3[:, gr, :], 0.0, None, ALU.max).then_inc(fin_sb, 1)

            layer_norm(0)
            relu_ff(0)
            layer_norm(1)
            relu_ff(1)
            layer_norm(2)
            shifts(0)
            layer_norm(3)
            shifts(1)
            shifts(2)
            finish(0)
            shifts(3)
            finish(1)

        @block.tensor
        def _(pe):
            mm = nc.tensor.matmul

            pe.wait_ge(tables_in["p0"], 16)
            for gr in range(GROUPS):
                v_bank = L0_BANKS[gr][2]
                for j in range(2):
                    pe.wait_ge(x_in[2 * gr + j], 16)
                    for n in range(2):
                        ins = mm(L0_BANKS[gr][n][64 * j:64 * j + 64, 0:TOK],
                                 table["wqk0"][:, 64 * n:64 * n + 64], xT[:, 2 * gr + j, :],
                                 start=True, stop=True)
                ins.then_inc(qk0_ps, 1)
                for j in range(2):
                    for b in range(BLK):
                        ins = mm(v_bank[:, (2 * j + b) * 128:(2 * j + b + 1) * 128],
                                 xT[:, 2 * gr + j, b * 128:b * 128 + 128], table["wv0_bd"],
                                 start=True, stop=True)
                ins.then_inc(v0_ps, 1)

            def scores(n):
                if n >= 3:
                    pe.wait_ge(exp_done, BLK * (n - 2))
                if n < IMAGES:
                    pe.wait_ge(q0_sb, n // 4 + 1)
                    pe.wait_ge(kz0_act, 2 * (n // 4 + 1))
                    pe.wait_ge(kz0_dve, 2 * (n // 4 + 1))
                    if n == 2:
                        pe.wait_ge(v0_sb, 2)
                    q, k = q0[:, n // 4, :], kz0[:, n, :]
                else:
                    m = n - IMAGES
                    pe.wait_ge(q1_sb, m // 4 + 1)
                    pe.wait_ge(k1_sb, 2 * (m // 4 + 1))
                    q, k = q1[:, m // 2, :], kz1[:, m, :]
                for b in range(BLK):
                    ins = mm(S_BANK[n % 3][:, b * TOK:(b + 1) * TOK], q[:, b * 128:b * 128 + 128], k,
                             start=True, stop=True)
                ins.then_inc(scores_ps, 1)

            def transposes(n):
                pe.wait_ge(norm_done, BLK * (n + 1))
                if n == 0:
                    pe.wait_ge(q0_sb, 2)
                    pe.wait_ge(kz0_act, 4)
                    pe.wait_ge(kz0_dve, 4)
                if n >= 2:
                    pe.wait_ge(probT_sb, n - 1)
                for mb in range(BLK):
                    for b in range(BLK):
                        ins = nc.tensor.transpose(T_BANK[n % 2][:, mb * TOK + b * 128:mb * TOK + b * 128 + 128],
                                                  probn[:, n % 2, b, mb * 128:mb * 128 + 128], ident)
                ins.then_inc(probT_ps, 1)

            def attend(p):
                j = p % PAIRS
                pe.wait_ge(probT_sb, 2 * p + 2)
                if p:
                    pe.wait_ge(attn_out, p)
                if p < PAIRS:
                    val = v0
                else:
                    pe.wait_ge(v1_sb, j // 2 + 1)
                    val = v1
                for mb in range(BLK):
                    for i in range(2):
                        ins = mm(O_BANK[64 * i:64 * i + 64, 0:TOK], val[:, 2 * j + mb, 64 * i:64 * i + 64],
                                 probT[:, (2 * p + i) % 4, mb, :], start=mb == 0, stop=mb == BLK - 1)
                ins.then_inc(pv_ps, 1)

            def prepare():
                pe.wait_ge(tables_in["p1"], 16)
                pe.wait_ge(tables_in["p2"], 16)
                pe.wait_ge(q0_sb, 1)
                b = W_BANK[0]
                mm(b[:, 0:128], table["wv1T_bd"], table["wo1_bd"], start=True, stop=True)
                mm(b[:, 128:256], table["outw_bd"], centre, start=True, stop=True)
                for h in range(FH):
                    mm(b[:, 256 + h * CH:256 + h * CH + CH], table["w2"][:, h * 128:h * 128 + 128],
                       centre[:, 0:CH], start=True, stop=True)
                for k, name in enumerate(("L2_conv_out_b", "L2_conv_b2")):
                    mm(b[:, 384 + k:385 + k], centre, col(name), start=True, stop=True)
                mm(b[:, 386:387], table["wo1_bd"], col("L1_conv_bv"), start=True, stop=True).then_inc(prep_ps, 1)

            def group_stats(gr):
                pe.wait_ge(stats_sb, gr + 1)
                if gr == 0:
                    pe.wait_ge(prep_sb, 1)
                    pe.wait_ge(kz0_act, 2)
                    pe.wait_ge(kz0_dve, 2)
                else:
                    pe.wait_ge(v1_sb, gr)
                mm(W_BANK[0][:, 0:4], table["pairavg"], flat(mv[:, 2 * gr:2 * gr + 2, :]),
                   start=True, stop=True).then_inc(gstats_ps, 1)

            def project1(gr):
                pe.wait_ge(h_ready, 2 * gr + 2)
                h2 = flat(hT[:, 2 * gr:2 * gr + 2, :])
                mm(W_BANK[0], table["wq1_bd"], h2, start=True, stop=True).then_inc(qkv1_ps, 1)
                if gr:
                    pe.wait_ge(k1_sb, 2 * gr)
                mm(W_BANK[1], table["wk1_bd"], h2, start=True, stop=True).then_inc(qkv1_ps, 1)

            def project1_values(gr):
                pe.wait_ge(q1_sb, gr + 1)
                for j in range(2):
                    for b in range(BLK):
                        ins = mm(W_BANK[0][:, (2 * j + b) * 128:(2 * j + b + 1) * 128],
                                 hT[:, 2 * gr + j, b * 128:b * 128 + 128], wvo1[:, :], start=True, stop=True)
                ins.then_inc(qkv1_ps, 1)

            def project2(gr, k, b):
                mm(b, inT[:, k, :], flat(zT[:, 2 * gr:2 * gr + 2, :]), start=True, stop=True)\
                    .then_inc(qkv2_ps, 1)

            def head_sums(gr):
                pe.wait_ge(prod_dve, 2 * gr + 2)
                pe.wait_ge(prod_pool, 2 * gr + 2)
                for k0, k1 in ((0, 4), (4, NB)):
                    for h in range(2):
                        for jp in range(2):
                            row = 64 * h + 32 * jp
                            ins = mm(duo[row:row + 32, k0 * 128:k1 * 128], head_sum[:, 16 - 16 * gr:48 - 16 * gr],
                                     qkprod[:, jp, k0:k1, 128 * h:128 * h + 128],
                                     start=gr == 0, stop=gr == GROUPS - 1)
                ins.then_inc(hexs_ps, 1)

            for n in range(SLOTS):
                if n in (7, 11):
                    group_stats(n // 4 - 1)
                if n < NATT:
                    scores(n)
                if n in (8, 12):
                    project1_values(n // 4 - 2)
                if n >= 4 and n % 2 == 0:
                    attend((n - 4) // 2)
                if 2 <= n < NATT + 2:
                    transposes(n - 2)
                if n == 3:
                    prepare()
                if n in (7, 11):
                    project1(n // 4 - 1)
                if n == 15:
                    pe.wait_ge(attn_out, PAIRS + 2)
                    pe.wait_ge(v1_sb, 2)
                    project2(0, 0, W_BANK[0])
                    pe.wait_ge(k1_sb, 4)
                    project2(0, 1, W_BANK[1])
                if n == 16:
                    pe.wait_ge(q2_sb, 1)
                    project2(0, 2, W_BANK[0])
            pe.wait_ge(attn_out, PAIRS + 4)
            pe.wait_ge(exp_done, BLK * NATT)
            for k in range(3):
                project2(1, k, S_BANK[k])
            pe.wait_ge(v2_sb, 1)
            pe.wait_ge(k2_sb, 1)
            head_sums(0)
            head_sums(1)

            def cast(m):
                j, h = m // 2, m % 2
                if m == 0:
                    pe.wait_ge(cast_r, 1)
                    pe.wait_ge(k2_sb, 2)
                    pe.wait_ge(q2_sb, 2)
                    pe.wait_ge(v2_sb, 2)
                    pe.wait_ge(probT_sb, NATT)
                if m >= 2:
                    pe.wait_ge(avprod_sb, m - 1)
                w = head_cast_r[:, 4 * h + 2 * (j % 2) + j // 2, :]
                for n, (k0, k1) in enumerate(((0, 3), (3, NB))):
                    if m == 0:
                        pe.wait_ge(att_ready, n + 1)
                    for a in (att_hi, att_lo):
                        ins = mm(CAST_BANKS[m % 2][n][:, 0:(k1 - k0) * 128], w, a[:, k0:k1, :],
                                 start=a is att_hi, stop=a is att_lo)
                ins.then_inc(cast_ps, 1)

            def out_proj(j):
                o = D_BANK[j // 2][:, TOK * (j % 2):TOK * (j % 2) + TOK]
                mm(o, centre, zT[:, j, :], start=True, stop=False)
                pe.wait_ge(avprod_sb, 2 * j + 2)
                mm(o, outc[:, :], avprod[:, j % 2, NB - 1, :], start=False, stop=False)
                pe.wait_ge(avsum_sb, j + 1)
                for k in range(NB // 2):
                    ins = mm(o, outc[:, :], avsum[:, j % 2, k, :], start=False, stop=k == NB // 2 - 1)
                ins.then_inc(av_used, 1)

            def variance(n):
                pe.wait_ge(sq_sb, n + 1)
                if n:
                    pe.wait_ge(lnv_sb, n)
                mm(bank[6], table["mean64"], sq[:, n % 2, :], start=True, stop=True).then_inc(var_ps, 1)

            def feed_forward1(gr):
                pe.wait_ge(ln_out, gr + 1)
                for h in range(FH):
                    for i in range(2):
                        m = 4 * gr + 2 * h + i
                        if gr:
                            pe.wait_ge(ff_act if i == 0 else ff_dve, h + 1)
                        mm(bank[m % 4], w1T[:, i, h, :], x1[:, gr, :], start=True, stop=True).then_inc(ff_ps, 1)

            def feed_forward2(gr):
                mm(D_BANK[gr], centre, x1[:, gr, :], start=True, stop=False)
                for h in range(FH):
                    pe.wait_ge(ff_act, 2 * gr + h + 1)
                    pe.wait_ge(ff_dve, 2 * gr + h + 1)
                    for i in range(2):
                        ins = mm(D_BANK[gr][64 * i:64 * i + 64, :], w2c[:, h, :], ffh[:, gr, h, i, :],
                                 start=False, stop=h == FH - 1)
                ins.then_inc(d_ps, 1)

            def conv1(c):
                gr, i = c // 2, c % 2
                pe.wait_ge(ln_out, 3 + gr)
                if c == 0:
                    pe.wait_ge(ff_act, 4)
                    pe.wait_ge(ff_dve, 4)
                mm(bank[c], c1[:, i, :], x2[:, gr, :], start=True, stop=True).then_inc(c1_ps, 1)

            def conv2(c):
                pe.wait_ge(shift_dve, 3 * (c + 1))
                pe.wait_ge(shift_pool, c + 1)
                if c == 1:
                    pe.wait_ge(lnv_sb, 4)
                if c >= 2:
                    pe.wait_ge(c2_sb, c - 1)
                for ty in range(3):
                    for r in range(CONV_BLOCKS):
                        ins = mm(bank[7 - c % 2][32 * r:32 * r + 32, :], ctap[:, r, ty, :],
                                 strips[:, c % 2, r, :, ty:ty + SIDE, :], start=ty == 0, stop=ty == 2)
                ins.then_inc(c2_ps, 1)

            def conv3(gr):
                for i in range(2):
                    pe.wait_ge(c2_sb, 2 * gr + i + 1)
                    ins = mm(D_BANK[gr][64 * i:64 * i + 64, :], table["c3"], c2out[:, gr, i, :],
                             start=True, stop=True)
                ins.then_inc(c3_ps, 1)

            cast(0)
            cast(1)
            for j in range(PAIRS):
                if j + 1 < PAIRS:
                    cast(2 * j + 2)
                    cast(2 * j + 3)
                if j == 2:
                    variance(0)
                out_proj(j)
            feed_forward1(0)
            variance(1)
            feed_forward2(0)
            feed_forward1(1)
            variance(2)
            feed_forward2(1)
            conv1(0)
            variance(3)
            conv1(1)
            conv2(0)
            conv1(2)
            conv2(1)
            conv1(3)
            conv3(0)
            conv2(2)
            conv2(3)
            conv3(1)


_OUT = "out_dram"


def packed_inputs(inputs):
    import numpy as np

    f = {k: np.asarray(v) for k, v in inputs.items()}
    part = {name: np.zeros((128, n), np.float32) for p in PACKS.values() for name, n in p}

    def diagonal(name, w):
        part[name][0:64, 0:64] = w
        part[name][64:128, 64:128] = w

    for i in range(2):
        for k, w in enumerate(("L0_conv_wq", "L0_conv_wk")):
            part["wqk0"][64 * i:64 * i + 64, 64 * k + 32 * i:64 * k + 32 * i + RC] = f[w]
    for k, b in enumerate(("L0_conv_bq", "L0_conv_bk")):
        for n in range(4):
            part["vcol"][32 * n:32 * n + RC, k] = f[b]
    for name in VEC64:
        part["vcol"][:, COL[name]] = np.concatenate([f[name], f[name]])
    for name in VEC128:
        part["vcol"][:, COL[name]] = f[name]
    for k in range(3):
        b = f["L2_conv_in_proj_b"][CH * k:CH * k + CH]
        part["vcol"][:, COL["in_proj_b"] + k] = np.concatenate([b, b])
    for h in range(FH):
        part["vcol"][:, COL["L2_conv_b1"] + h] = f["L2_conv_b1"][128 * h:128 * h + 128]
    diagonal("wv0_bd", f["L0_conv_wv"])
    diagonal("wq1_bd", f["L1_conv_Wq"])
    diagonal("wk1_bd", f["L1_conv_Wk"])
    diagonal("wv1T_bd", f["L1_conv_Wv"].T)
    diagonal("wo1_bd", f["L1_conv_Wo"])
    diagonal("outw_bd", f["L2_conv_out_w"])
    for k in range(3):
        w = f["L2_conv_in_proj_w"][CH * k:CH * k + CH].T
        for i in range(2):
            part["inT_bd"][64 * i:64 * i + 64, 128 * k + 64 * i:128 * k + 64 * i + 64] = w
    for i in range(2):
        part["w1T"][64 * i:64 * i + 64, DFF * i:DFF * i + DFF] = f["L2_conv_w1"].T
        part["c1"][64 * i:64 * i + 64, CM * i:CM * i + CM] = f["L3_conv_w1"][0, 0]
    part["w2"][0:CH, :] = f["L2_conv_w2"]
    part["c3"][:, :] = f["L3_conv_w3"][0, 0]
    for r in range(CONV_BLOCKS):
        for ty in range(3):
            for tx in range(3):
                for g in range(8):
                    at = 32 * (3 * r + ty) + 4 * g
                    m = 32 * r + 4 * g
                    part["ctap"][32 * tx + 4 * g:32 * tx + 4 * g + 4, at:at + 4] = \
                        f["L3_conv_w2"][ty, tx, :, m:m + 4]
    eye = np.eye(128, dtype=np.float32)
    part["ident"][:, :] = eye
    part["pairavg"][:, :] = np.kron(np.eye(64), np.full((2, 2), 0.5))
    part["mean64"][:, :] = np.kron(np.eye(2), np.full((64, 64), 1.0 / CH))
    part["centre"][:, :] = np.eye(128) - np.kron(np.eye(2), np.full((64, 64), 1.0 / CH))
    part["head_sum"][:, 16:32] = np.kron(np.eye(16), np.ones((HD, 1)))
    arrays = {p: np.concatenate([part[name] for name, _ in parts], axis=1) for p, parts in PACKS.items()}
    x = f["x"].reshape(PAIRS, 2, TOK, CH)
    arrays["xT"] = np.ascontiguousarray(x.transpose(1, 3, 0, 2).reshape(128, PAIRS * TOK))
    return arrays


def kernel(**inputs):
    import numpy as np
    import concourse.bacc as bacc
    from concourse.bass_utils import run_bass_kernel_spmd

    nc = bacc.Bacc("TRN2", target_bir_lowering=False, num_devices=1)
    arrays = packed_inputs(inputs)
    aps = {name: nc.dram_tensor(f"in_{name}", a.shape, F32, kind="ExternalInput").ap()
           for name, a in arrays.items()}
    out = nc.dram_tensor(_OUT, (128, PAIRS * TOK), F32, kind="ExternalOutput").ap()
    build(nc, aps, out)
    r = run_bass_kernel_spmd(nc, [{f"in_{n}": a for n, a in arrays.items()}], core_ids=[0])
    y = np.asarray(r.results[0][_OUT]).reshape(2, CH, PAIRS, TOK)
    return np.ascontiguousarray(y.transpose(2, 0, 3, 1).reshape(IMAGES, SIDE, SIDE, CH))
```

```python
from contextlib import ExitStack

import concourse.bass as bass
from concourse import mybir

F32 = mybir.dt.float32
F32R = mybir.dt.float32r
ALU = mybir.AluOpType
ACT = mybir.ActivationFunctionType
AX = mybir.AxisListType

IMAGES, SIDE, CH = 8, 16, 64
TOK = SIDE * SIDE
PAIRS = IMAGES // 2
GROUPS = PAIRS // 2
BLK = TOK // 128
RC = CH // 8
HEADS, HD = 8, 8
DFF = 256
FH = DFF // 128
CM = 128
PAD = SIDE + 2
HEX_RUNS = [[(-1, 0), (0, 0), (1, 0)], [(0, -1), (0, 1)], [(1, -1), (-1, 1)]]
NB = sum(len(run) for run in HEX_RUNS)
EPS_GN, EPS_LN, EPS_BN = 1e-6, 1e-5, 1e-3

VEC64 = ["L1_conv_gn_scale", "L1_conv_gn_bias", "L1_conv_bq", "L1_conv_bk", "L1_conv_bv",
         "L0_conv_bv", "L1_conv_bo", "L2_conv_out_b", "L2_conv_b2",
         "L2_conv_g1", "L2_conv_beta1", "L2_conv_g2", "L2_conv_beta2", "L3_conv_b3"]
VEC128 = ["L3_conv_b1", "L3_conv_g1", "L3_conv_be1", "L3_conv_m1", "L3_conv_v1",
          "L3_conv_b2", "L3_conv_g2", "L3_conv_be2", "L3_conv_m2", "L3_conv_v2"]
COL = {"L0_conv_bq": 0, "L0_conv_bk": 1}
for _name in VEC64 + VEC128:
    COL[_name] = len(COL)
COL["in_proj_b"] = len(COL)
COL["L2_conv_b1"] = len(COL) + 2
COLS = COL["L2_conv_b1"] + FH

STRIPS, CONV_BLOCKS = 4, CM // 32
PACKS = {
    "p0": [("wqk0", 128), ("vcol", COLS)],
    "pv": [("wv0_bd", 128), ("ident", 128)],
    "p1": [("wq1_bd", 128), ("wk1_bd", 128), ("wv1T_bd", 128), ("wo1_bd", 128), ("pairavg", 128),
           ("centre", 128), ("pairdiff", 128)],
    "p2": [("inT_bd", 3 * 128), ("outw_bd", 128), ("w1T", DFF), ("w2", DFF),
           ("mean64", 128), ("head_sum", 48), ("c1", 2 * CM), ("ctap", CONV_BLOCKS * 3 * 32), ("c3", CH)],
}


def pack_width(pack):
    return sum(n for _, n in PACKS[pack])


def build(nc, t, out):
    ctx = ExitStack()
    with ctx:
        def sb(name, *shape):
            return ctx.enter_context(nc.sbuf_tensor(name, list(shape), F32))

        def sem(name):
            return ctx.enter_context(nc.semaphore(name))

        low = [ctx.enter_context(nc.psum_tensor(f"bank{i}", [128, 512], F32)) for i in range(6)]
        duo = ctx.enter_context(nc.psum_tensor("duo", [128, 1024], F32))
        bank = [b[:, :] for b in low] + [duo[:, 0:512], duo[:, 512:1024]]
        S_BANK = bank[0:3]
        T_BANK = bank[3:5]
        O_BANK = bank[5]
        W_BANK = bank[6:8]
        CAST_BANKS = [(bank[0], bank[1]), (bank[2], bank[3])]
        D_BANK = bank[4:6]

        head_cast = sb("head_cast", 128, 2 * PAIRS, 128)
        head_cast_r = ctx.enter_context(nc.sbuf_tensor("head_cast_r", [128, 2 * PAIRS, 128], F32R))
        epsln = sb("epsln", 128, 1)
        minus_half = sb("minus_half", 128, 4)
        epsgn = sb("epsgn", 128, 3)
        zeros = sb("zeros", 128, 2 * PAD * PAD)
        packed = {p: sb(p, 128, pack_width(p)) for p in PACKS}
        table = {}
        for p, parts in PACKS.items():
            at = 0
            for name, n in parts:
                table[name] = packed[p][:, at:at + n]
                at += n
        vcol, ident, centre = table["vcol"], table["ident"], table["centre"]
        inT = table["inT_bd"].rearrange("p (k m) -> p k m", k=3)
        head_sum = table["head_sum"]
        c1 = table["c1"].rearrange("p (i m) -> p i m", i=2)
        ctap = table["ctap"].rearrange("p (r t m) -> p r t m", r=CONV_BLOCKS, t=3)
        wvo1 = sb("wvo1", 128, 128)
        outc = sb("outc", 128, 128)
        w2c = sb("w2c", 128, FH, CH)
        cb = sb("cb", 128, 3)
        qb8 = sb("qb8", 128, 1)
        bnv = sb("bnv", 128, 2)
        bnr = sb("bnr", 128, 2)
        bninv = sb("bninv", 128, 2)
        c1s = sb("c1s", 128, 2, CM)
        centre_r = ctx.enter_context(nc.sbuf_tensor("centre_r", [128, 2, 128], F32R))
        ctaps = sb("ctaps", 128, CONV_BLOCKS, 3, 32)
        bnsh = sb("bnsh", 128, 2)
        xT = sb("xT", 128, PAIRS, TOK)
        q0 = sb("q0", 128, GROUPS, TOK)
        kz0 = sb("kz0", 128, IMAGES, TOK)
        v0 = sb("v0", 128, PAIRS * BLK, 128)
        prob = sb("prob", 128, 3, BLK, TOK)
        probn = sb("probn", 128, 2, BLK, TOK)
        probT = sb("probT", 128, 4, BLK, TOK)
        nmax = sb("nmax", 128, 2 * IMAGES, BLK)
        rsum = sb("rsum", 128, 2 * IMAGES, BLK)
        rrec = sb("rrec", 128, 2 * IMAGES, BLK)
        yT = sb("yT", 128, PAIRS, TOK)
        bnst = sb("bnst", 128, PAIRS, 6)
        mv = sb("mv", 128, PAIRS, 2)
        gmv = sb("gmv", 128, PAIRS, 3)
        gvar = sb("gvar", 128, PAIRS)
        grs = sb("grs", 128, PAIRS)
        gsc = sb("gsc", 128, PAIRS)
        gbi = sb("gbi", 128, PAIRS)
        hT = sb("hT", 128, PAIRS, TOK)
        q1 = sb("q1", 128, PAIRS, TOK)
        kz1 = sb("kz1", 128, IMAGES, TOK)
        v1 = sb("v1", 128, PAIRS * BLK, 128)
        zT = sb("zT", 128, PAIRS, TOK)
        q2 = sb("q2", 128, PAIRS, TOK)
        k2 = sb("k2", 128, PAIRS, PAD, PAD)
        v2 = sb("v2", 128, PAIRS, PAD, PAD)
        qkprod = sb("qkprod", 128, 2, NB, TOK)
        smax = sb("smax", 128, 2, 64)
        ssum = sb("ssum", 128, 2, 64)
        sexp = sb("sexp", 128, 2, NB, 64)
        att = sb("att", 128, 2, NB, 64)
        att_hi = ctx.enter_context(nc.sbuf_tensor("att_hi", [128, 2, NB, 64], F32R))
        att_lo = ctx.enter_context(nc.sbuf_tensor("att_lo", [128, 2, NB, 64], F32R))
        avsum = sb("avsum", 128, 2, NB // 2, TOK)
        w1_hi = ctx.enter_context(nc.sbuf_tensor("w1_hi", [128, DFF], F32R))
        w1_lo = ctx.enter_context(nc.sbuf_tensor("w1_lo", [128, DFF], F32R))
        xs = ctx.enter_context(nc.sbuf_tensor("xs", [128, GROUPS, 2, 512], F32R))
        sq = sb("sq", 128, 2, 512)
        lnv = sb("lnv", 128, 2, 512)
        rstd = sb("rstd", 128, 2, 512)
        xhat = sb("xhat", 128, 2, 512)
        x1 = sb("x1", 128, GROUPS, 512)
        x2 = yT[:, :, :].rearrange("p (g j) n -> p g (j n)", g=GROUPS)
        ffh = sb("ffh", 128, 2, FH, 2, 512)
        strips = sb("strips", 128, 2, CONV_BLOCKS, 2, PAD, SIDE)
        products = [qkprod[:, 0, :, :], qkprod[:, 1, :, :]] + [
            ffh[:, i, :, :, :].rearrange("p a b c -> p (a b c)")[:, 0:NB * TOK]
            .rearrange("p (k n) -> p k n", k=NB) for i in range(2)]
        prob2 = prob[:, :, :, :].rearrange("p a b n -> p (a b n)").rearrange("p (i k n) -> p i k n", i=2, n=TOK)
        value_sums = [avsum[:, 0, :, :], avsum[:, 1, :, :], prob2[:, 0, :, :], prob2[:, 1, :, :]]
        c2out = ffh[:, 0, :, :, :]
        x3 = sq[:, :, :].rearrange("p a n -> p (a n)")
        fin = xT[:, :, :].rearrange("p j n -> p (j n)")

        x_in = [sem(f"x_in{j}") for j in range(PAIRS)]
        tables_in = {p: sem(f"{p}_in") for p in PACKS}
        stored = sem("stored")
        zeros_ready = sem("zeros_ready")
        zeroed = sem("zeroed")
        consts = sem("consts")
        eps_ready = sem("eps_ready")
        pool_step = sem("pool_step")
        dve_step = sem("dve_step")
        qb8_ready = sem("qb8_ready")
        prep_ps = sem("prep_ps")
        prep_sb = sem("prep_sb")
        prep2_ps, prep2_sb = sem("prep2_ps"), sem("prep2_sb")
        qk0_ps, q0_sb = sem("qk0_ps"), sem("q0_sb")
        kz0_act, kz0_dve = sem("kz0_act"), sem("kz0_dve")
        v0_ps, v0_sb = sem("v0_ps"), sem("v0_sb")
        scores_ps = sem("scores_ps")
        max_ready = sem("max_ready")
        exp_done = sem("exp_done")
        norm_done = sem("norm_done")
        probT_ps, probT_sb = sem("probT_ps"), sem("probT_sb")
        pv_ps = sem("pv_ps")
        attn_out = sem("attn_out")
        stats_sb, gstats_ps, gstats_sb = sem("stats_sb"), sem("gstats_ps"), sem("gstats_sb")
        gvar_ready, grs_ready = sem("gvar_ready"), sem("grs_ready")
        h_ready = sem("h_ready")
        qkv1_ps, q1_sb, k1_sb, v1_sb = sem("qkv1_ps"), sem("q1_sb"), sem("k1_sb"), sem("v1_sb")
        kv2_border = sem("kv2_border")
        qkv2_ps, q2_sb, k2_sb, v2_sb = sem("qkv2_ps"), sem("q2_sb"), sem("k2_sb"), sem("v2_sb")
        prod_dve, prod_pool = sem("prod_dve"), sem("prod_pool")
        hexs_ps, cast_r = sem("hexs_ps"), sem("cast_r")
        hex_shift, hex_exp = sem("hex_shift"), sem("hex_exp")
        att_f32, att_upper = sem("att_f32"), sem("att_upper")
        att_lower0, att_lower1 = sem("att_lower0"), sem("att_lower1")
        cast_ps, avprod_sb, avsum_sb = sem("cast_ps"), sem("avprod_sb"), sem("avsum_sb")
        av_used, avsum_part = sem("av_used"), sem("avsum_part")
        d_ps, sq_sb, var_ps = sem("d_ps"), sem("sq_sb"), sem("var_ps")
        lnv_sb, rstd_sb = sem("lnv_sb"), sem("rstd_sb")
        xhat_sb, ln_out = sem("xhat_sb"), sem("ln_out")
        stacked = sem("stacked")
        w1_split, x_upper, x_lower = sem("w1_split"), sem("x_upper"), sem("x_lower")
        ff_ps, ff_act, ff_dve = sem("ff_ps"), sem("ff_act"), sem("ff_dve")
        c1_ps, c1_sb, c2_ps, c2_sb = sem("c1_ps"), sem("c1_sb"), sem("c2_ps"), sem("c2_sb")
        shifted = sem("shifted")
        bn_ready, bnrow_ps, taps_ready = sem("bn_ready"), sem("bnrow_ps"), sem("taps_ready")
        c3_ps, fin_sb = sem("c3_ps"), sem("fin_sb")

        def col(name, k=0):
            r = COL[name] + k
            return vcol[:, r:r + 1]

        def hexview(buf, j, run, rows=SIDE, row0=0):
            (q0, r0), (q1_, r1_) = run[0], run[1]
            step = (r1_ - r0) * PAD + (q1_ - q0)
            base = buf[:, j, 1 + r0 + row0:1 + r0 + row0 + rows, 1 + q0:1 + q0 + SIDE]
            a = [list(x) for x in base.ap]
            return bass.AP(tensor=base.tensor, offset=base.offset,
                           ap=[a[0], [step, len(run)]] + a[1:])

        def rep(ap, n):
            a = [list(x) for x in ap.ap]
            return bass.AP(tensor=ap.tensor, offset=ap.offset, ap=[a[0], [0, n]] + a[1:])

        def key_product(engine, j, r):
            k0, n = RUN_START[r], len(HEX_RUNS[r])
            return engine.tensor_tensor(
                products[j][:, k0:k0 + n, :].rearrange("p k (a b) -> p k a b", b=SIDE),
                rep(q2[:, j, :].rearrange("p (a b) -> p a b", b=SIDE), n),
                hexview(k2, j, HEX_RUNS[r]), ALU.mult)

        def att_lower_halves(engine, c):
            return engine.tensor_tensor(att_lo[:, c, :, :], att[:, c, :, :], att_hi[:, c, :, :].bitcast(F32),
                                        ALU.subtract)

        block = ctx.enter_context(nc.Block())

        NATT = 2 * IMAGES
        SLOTS = NATT + 3
        QK2_SLOTS, V2_SLOTS = (13, 15, 17, 18), (14, 16, 17, 18)
        L0_BANKS = (bank[6], bank[7], bank[5])
        PREP_BANK = bank[3]
        RESULTS = [(bank[4], slice(0, 512))] + \
            [(bank[2 + h][:, 0:TOK], slice(512 + TOK * h, 512 + TOK * h + TOK)) for h in range(2)]
        WARM_UP, WARM_SOFTMAX, WARM_SOFTMAX2 = 1, 2, 1
        PREPARE = 3

        OUT_BANK = [O_BANK] * (NATT // 2 - 1) + [T_BANK[0]]

        PROJ2 = [(bank[6], bank[7], bank[6])] * 2 + [(bank[1], bank[2], bank[0])] * 2

        POOL_RUNS = [(0, 2), (0, 2), (2,), (2,)]
        RUN_START = [0, 3, 5]
        SEVENTH_ADDED = (0, 1, 2)

        UNITS = [(0, 0), (1, 0), (0, 1), (1, 1), (2, 0), (2, 1), (3, 0), (3, 1)]
        LAST_UNIT = [3, 4, 6, 8]

        AFFINE = [("L2_conv_g1", "L2_conv_beta1"), ("L2_conv_g2", "L2_conv_beta2")]

        def flat(ap):
            return ap.rearrange("p a b -> p (a b)")

        def shift(engine, c, r, s):
            d, f = (slice(1, SIDE), slice(0, SIDE - 1)) if s == 0 else (slice(0, SIDE - 1), slice(1, SIDE))
            return engine.tensor_copy(strips[32 * s:32 * s + 32, c % 2, r, :, 1:1 + SIDE, d],
                                      strips[32:64, c % 2, r, :, 1:1 + SIDE, f])

        @block.sync
        def _(sp):
            xd = t["xT"].rearrange("p (j n) -> p j n", j=PAIRS)
            for j in range(PAIRS):
                sp.dma_start(xT[:, j, :], xd[:, j, :]).then_inc(x_in[j], 16)
            sp.dma_start(packed["p2"][:, :], t["p2"]).then_inc(tables_in["p2"], 16)
            for n, (b, columns) in enumerate(RESULTS):
                sp.wait_ge(fin_sb, n + 1)
                sp.dma_start(out[:, columns], fin[:, columns]).then_inc(stored, 16)
            sp.wait_ge(stored, 16 * len(RESULTS))

        @block.gpsimd
        def _(pool):
            g = nc.gpsimd
            g.memset(flat(kz0[:, :, :]), 0.0).then_inc(zeroed, 1)
            g.memset(flat(kz1[:, :, :]), 0.0).then_inc(zeroed, 1)
            g.memset(strips[:, :, :, :, :, :].rearrange("p a b c d e -> p (a b c d e)"), 0.0)\
                .then_inc(zeroed, 1)
            g.memset(flat(head_cast[:, :, :]), 0.0).then_inc(pool_step, 1)
            g.memset(minus_half[:, :], -0.5).then_inc(pool_step, 1)
            g.memset(epsln[:, :], EPS_LN).then_inc(pool_step, 1)
            g.memset(epsgn[:, :], 0.0).then_inc(pool_step, 1)
            pool.wait_ge(pool_step, 4)
            g.memset(epsgn[:, 1:2], EPS_GN).then_inc(eps_ready, 1)
            v = head_cast[:, :, :].rearrange("p u (a b) -> p u a b", b=HD)
            g.affine_select(out=v, in_=v, compare_op=ALU.not_equal, fill=1.0, base=0,
                            pattern=[[-16, 2 * PAIRS], [-1, 16], [0, HD]], channel_multiplier=1)\
                .then_inc(consts, 1)

            pool.wait_ge(tables_in["p0"], 16)
            pool.wait_ge(zeros_ready, 1)
            borders = [(buf, k, h) for buf, k in ((k2, 1), (v2, 2)) for h in range(GROUPS)]
            for j in range(PAIRS):
                pool.wait_ge(gvar_ready, j + 1)
                g.tensor_tensor(grs[:, j:j + 1], gvar[:, j:j + 1], minus_half[:, 0:1], ALU.pow)\
                    .then_inc(grs_ready, 1)
                buf, k, h = borders[j]
                g.tensor_scalar(buf[:, 2 * h:2 * h + 2, :, :].rearrange("p a b c -> p (a b c)"),
                                zeros[:, :], col("in_proj_b", k), None, ALU.add).then_inc(kv2_border, 1)

            pool.wait_ge(bn_ready, 1)
            g.tensor_tensor(bnr[:, :], bnv[:, :], minus_half[:, 0:2], ALU.pow).then_inc(bn_ready, 1)

            for j in range(PAIRS):
                pool.wait_ge(q2_sb, j + 1)
                pool.wait_ge(k2_sb, j + 1)
                for r in POOL_RUNS[j]:
                    ins = key_product(g, j, r)
                ins.then_inc(prod_pool, 1)
            pool.wait_ge(att_upper, 2)
            att_lower_halves(g, 1).then_inc(att_lower1, 1)
            for m, (j, c) in enumerate(UNITS):
                pool.wait_ge(avprod_sb, m + 1)
                total, terms = [b.rearrange("p k (h c n) -> p k h c n", h=2, c=2)[:, :, :, c, :]
                                for b in (value_sums[j], products[j])]
                ins = g.tensor_tensor(total, terms[:, 0:NB - 1:2, :, :], terms[:, 1:NB - 1:2, :, :], ALU.add)
                if j in SEVENTH_ADDED:
                    ins.then_inc(avsum_part, 1)
                    pool.wait_ge(avsum_part, m + 1)
                    ins = g.tensor_tensor(total[:, 2, :, :], total[:, 2, :, :], terms[:, NB - 1, :, :], ALU.add)
                ins.then_inc(avsum_sb, 1)

        @block.scalar
        def _(act):
            s = nc.scalar
            for p in ("p0", "pv", "p1"):
                act.dma_start(packed[p][:, :], t[p]).then_inc(tables_in[p], 16)
            s.preload_act_table_set("natural_log_exp_and_others")
            act.wait_ge(tables_in["p0"], 16)
            s.activation(qb8[:, :], col("L1_conv_bq"), ACT.Copy, scale=CH ** -0.5).then_inc(qb8_ready, 1)
            act.wait_ge(zeroed, 1)

            def queries0(gr):
                act.wait_ge(qk0_ps, gr + 1)
                qb = L0_BANKS[0]
                s.activation(q0[:, gr, :], qb[:, 0:TOK], ACT.Relu, bias=col("L0_conv_bq")).then_inc(q0_sb, 1)

            def keys0(gr):
                kb = L0_BANKS[1]
                for n in range(2):
                    h = slice(32 * n, 32 * n + 32)
                    s.activation(kz0[h, 4 * gr + n, :], kb[h, 0:TOK], ACT.Relu,
                                 bias=col("L0_conv_bk")[h]).then_inc(kz0_act, 1)

            queries0(0)
            keys0(0)

            def exps(n):
                act.wait_ge(max_ready, n + 1)
                if n >= 3:
                    act.wait_ge(norm_done, BLK * (n - 2))
                for b in range(BLK):
                    s.activation(prob[:, n % 3, b, :], S_BANK[n % 3][:, b * TOK:(b + 1) * TOK], ACT.Exp,
                                 bias=nmax[:, n, b:b + 1], accum_out=rsum[:, n, b:b + 1]).then_inc(exp_done, 1)

            def copy_probT(n):
                act.wait_ge(probT_ps, n + 1)
                if n >= 4:
                    act.wait_ge(pv_ps, n // 2 - 1)
                s.activation(flat(probT[:, n % 4, :, :]), T_BANK[n % 2], ACT.Copy).then_inc(probT_sb, 1)

            def keys_queries1(j):
                if j == 0:
                    act.wait_ge(qb8_ready, 1)
                    act.wait_ge(zeroed, 2)
                act.wait_ge(qkv1_ps, 3 * j + 1)
                s.activation(q1[:, j, :], W_BANK[0][:, 0:TOK], ACT.Identity, bias=qb8[:, :],
                             scale=CH ** -0.5).then_inc(q1_sb, 1)
                act.wait_ge(qkv1_ps, 3 * j + 2)
                for i in range(2):
                    h = slice(64 * i, 64 * i + 64)
                    s.activation(kz1[h, 2 * j + i, :], W_BANK[1][h, 0:TOK], ACT.Identity,
                                 bias=col("L1_conv_bk")[h]).then_inc(k1_sb, 1)

            def values1(j):
                act.wait_ge(qkv1_ps, 3 * j + 3)
                s.activation(flat(v1[:, 2 * j:2 * j + 2, :]), W_BANK[0][:, 0:TOK], ACT.Copy).then_inc(v1_sb, 1)

            def keys_queries2(j):
                act.wait_ge(kv2_border, 4)
                act.wait_ge(qkv2_ps, 3 * j + 1)
                s.activation(q2[:, j, :], PROJ2[j][0][:, 0:TOK], ACT.Identity, bias=col("in_proj_b", 0))\
                    .then_inc(q2_sb, 1)
                act.wait_ge(qkv2_ps, 3 * j + 2)
                s.activation(k2[:, j, 1:1 + SIDE, 1:1 + SIDE],
                             PROJ2[j][1][:, 0:TOK].rearrange("p (a b) -> p a b", b=SIDE),
                             ACT.Identity, bias=col("in_proj_b", 1)).then_inc(k2_sb, 1)

            def values2(j):
                act.wait_ge(qkv2_ps, 3 * j + 3)
                s.activation(v2[:, j, 1:1 + SIDE, 1:1 + SIDE],
                             PROJ2[j][2][:, 0:TOK].rearrange("p (a b) -> p a b", b=SIDE),
                             ACT.Identity, bias=col("in_proj_b", 2)).then_inc(v2_sb, 1)

            for n in range(SLOTS):
                if n in (7, 9, 11, 13):
                    values1((n - 7) // 2)
                if n < NATT:
                    exps(n)
                if n == 1:
                    queries0(1)
                if n == 2:
                    keys0(1)
                if n in (6, 8, 10, 12):
                    keys_queries1(n // 2 - 3)
                if 2 <= n <= NATT:
                    copy_probT(n - 2)
                if n == NATT:
                    copy_probT(n - 1)
                if n in QK2_SLOTS:
                    keys_queries2(QK2_SLOTS.index(n))
                if n in V2_SLOTS:
                    values2(V2_SLOTS.index(n))

            act.wait_ge(tables_in["p1"], 16)
            for i in range(2):
                for half in range(2):
                    h = slice(64 * half, 64 * half + 64)
                    ins = s.activation(centre_r[h, i, :], centre[64 * i:64 * i + 64, :], ACT.Copy)
            ins.then_inc(stacked, 1)

            for c in range(2):
                act.wait_ge(hex_shift, c + 1)
                s.activation(flat(sexp[:, c, :, :]), flat(sexp[:, c, :, :]), ACT.Exp,
                             scale=float(HD) ** -0.5).then_inc(hex_exp, 1)
                if c == 0:
                    act.wait_ge(prep2_ps, 1)
                    s.activation(outc[:, :], PREP_BANK[:, 0:128], ACT.Copy)
                    s.activation(flat(w2c[:, :, :]), PREP_BANK[:, 128:256], ACT.Copy)
                    s.activation(cb[:, 0:2], PREP_BANK[:, 256:258], ACT.Copy).then_inc(prep2_sb, 1)
                act.wait_ge(att_f32, c + 1)
                s.activation(flat(att_hi[:, c, :, :]), flat(att[:, c, :, :]), ACT.Copy).then_inc(att_upper, 1)

            def squares(n):
                if n < 2:
                    act.wait_ge(av_used, 2 * n + 2)
                else:
                    act.wait_ge(d_ps, n - 1)
                    act.wait_ge(var_ps, n - 1)
                s.activation(sq[:, n % 2, :], D_BANK[n % 2], ACT.Square, bias=cb[:, n // 2:n // 2 + 1])\
                    .then_inc(sq_sb, 1)

            def inverse_std(n):
                act.wait_ge(var_ps, n + 1)
                s.activation(lnv[:, n % 2, :], bank[6], ACT.Ln, bias=epsln[:, :]).then_inc(lnv_sb, 1)
                act.wait_ge(lnv_sb, n + 1)
                if n >= 2:
                    act.wait_ge(xhat_sb, n - 1)
                s.activation(rstd[:, n % 2, :], lnv[:, n % 2, :], ACT.Exp, scale=-0.5).then_inc(rstd_sb, 1)

            def relu_ff(gr):
                for h in range(FH):
                    act.wait_ge(ff_ps, 2 * FH * gr + h + 1)
                    s.activation(ffh[:, gr, h, 0, :], bank[h], ACT.Relu,
                                 bias=col("L2_conv_b1", h)).then_inc(ff_act, 1)

            def conv1_out(c):
                act.wait_ge(c1_ps, c + 1)
                if c == 0:
                    act.wait_ge(bn_ready, 3)
                    act.wait_ge(zeroed, 3)
                if c >= 2:
                    act.wait_ge(c2_ps, c - 1)
                for r in range(CONV_BLOCKS):
                    h = slice(32 * r, 32 * r + 32)
                    s.activation(strips[32:64, c % 2, r, :, 1:1 + SIDE, :],
                                 bank[c][h, :].rearrange("p (j a b) -> p j a b", j=2, b=SIDE),
                                 ACT.Relu, bias=bnsh[h, 0:1]).then_inc(c1_sb, 1)

            def conv2_out_last():
                for h in range(2):
                    act.wait_ge(c2_ps, 4 + h)
                    s.activation(c2out[:, 1, 1, TOK * h:TOK * h + TOK], bank[h][:, 0:TOK], ACT.Relu,
                                 bias=bnsh[:, 1:2]).then_inc(c2_sb, 1)

            def conv2_out(c):
                act.wait_ge(c2_ps, c + 1)
                s.activation(c2out[:, c // 2, c % 2, :], bank[7 - c % 2], ACT.Relu,
                             bias=bnsh[:, 1:2]).then_inc(c2_sb, 1)

            act.wait_ge(consts, 1)
            squares(0)
            inverse_std(0)
            squares(1)
            inverse_std(1)
            relu_ff(0)
            squares(2)
            inverse_std(2)
            relu_ff(1)
            squares(3)
            conv1_out(0)
            inverse_std(3)
            conv1_out(1)
            conv2_out(0)
            conv1_out(2)
            conv1_out(3)
            conv2_out(1)
            conv2_out(2)
            conv2_out_last()

        @block.vector
        def _(dve):
            v = nc.vector
            step = [0]

            def done(ins):
                step[0] += 1
                ins.then_inc(dve_step, 1)
                dve.wait_ge(dve_step, step[0])

            v.memset(zeros[:, :], 0.0).then_inc(zeros_ready, 1)
            dve.wait_ge(tables_in["p0"], 16)
            dve.wait_ge(zeroed, 1)

            def keys0(gr):
                dve.wait_ge(qk0_ps, gr + 1)
                for n in range(2, 4):
                    h = slice(32 * n, 32 * n + 32)
                    v.tensor_scalar(kz0[h, 4 * gr + n, :], L0_BANKS[1][h, 0:TOK],
                                    col("L0_conv_bk")[h], 0.0, ALU.add, ALU.max).then_inc(kz0_dve, 1)

            def values0(gr):
                dve.wait_ge(v0_ps, gr + 1)
                v.tensor_copy(flat(v0[:, 4 * gr:4 * gr + 4, :]), L0_BANKS[2]).then_inc(v0_sb, 1)

            keys0(0)
            values0(0)

            def maxes(n):
                dve.wait_ge(scores_ps, n + 1)
                v.tensor_reduce(nmax[:, n, :], S_BANK[n % 3].rearrange("p (b m) -> p b m", b=BLK),
                                AX.X, ALU.max, negate=True).then_inc(max_ready, 1)

            def normalise(n):
                dve.wait_ge(exp_done, BLK * (n + 1))
                done(v.reciprocal(rrec[:, n, :], rsum[:, n, :]))
                if n >= 2:
                    dve.wait_ge(probT_ps, n - 1)
                for b in range(BLK):
                    v.tensor_scalar(probn[:, n % 2, b, :], prob[:, n % 3, b, :], rrec[:, n, b:b + 1], None,
                                    ALU.mult).then_inc(norm_done, 1)

            def residual(p):
                j = p % PAIRS
                dve.wait_ge(pv_ps, p + 1)
                bias, src, dst = (col("L0_conv_bv"), xT, yT) if p < PAIRS else (cb[:, 2:3], yT, zT)
                v.scalar_tensor_tensor(out=dst[:, j, :], in0=OUT_BANK[p][:, 0:TOK], scalar=bias, in1=src[:, j, :],
                                       op0=ALU.add, op1=ALU.add).then_inc(attn_out, 1)

            def stats(j):
                dve.wait_ge(attn_out, j + 1)
                done(v.bn_stats(bnst[:, j, :], yT[:, j, :]))
                v.bn_aggr(mv[:, j, :], bnst[:, j, :]).then_inc(stats_sb, 1)

            def group_variance(j):
                dve.wait_ge(gstats_ps, j + 1)
                dve.wait_ge(eps_ready, 1)
                v.tensor_tensor(gmv[:, j, :], O_BANK[:, 0:3], epsgn[:, :], ALU.add).then_inc(gstats_sb, 1)
                dve.wait_ge(gstats_sb, j + 1)
                v.scalar_tensor_tensor(out=gvar[:, j:j + 1], in0=gmv[:, j, 2:3], scalar=gmv[:, j, 2:3],
                                       in1=gmv[:, j, 1:2], op0=ALU.mult, op1=ALU.add).then_inc(gvar_ready, 1)

            def group_norm(j):
                dve.wait_ge(grs_ready, j + 1)
                done(v.tensor_scalar(gsc[:, j:j + 1], grs[:, j:j + 1], col("L1_conv_gn_scale"), None, ALU.mult))
                done(v.scalar_tensor_tensor(out=gbi[:, j:j + 1], in0=gmv[:, j, 0:1], scalar=gsc[:, j:j + 1],
                                            in1=col("L1_conv_gn_bias"), op0=ALU.mult, op1=ALU.subtract))
                v.tensor_scalar(hT[:, j, :], yT[:, j, :], gsc[:, j:j + 1], gbi[:, j:j + 1],
                                ALU.mult, ALU.subtract).then_inc(h_ready, 1)

            def prepared():
                dve.wait_ge(prep_ps, 1)
                v.tensor_copy(wvo1[:, :], W_BANK[0][:, 0:128])
                v.tensor_tensor(cb[:, 2:3], W_BANK[0][:, 128:129], col("L1_conv_bo"), ALU.add)\
                    .then_inc(prep_sb, 1)

            def batch_norm_variances():
                for k, nm in enumerate(("L3_conv_v1", "L3_conv_v2")):
                    ins = v.tensor_scalar(bnv[:, k:k + 1], col(nm), EPS_BN, None, ALU.add)
                ins.then_inc(bn_ready, 1)

            def batch_norm():
                dve.wait_ge(bn_ready, 2)
                for k, (gm, b, mn, be) in enumerate((("L3_conv_g1", "L3_conv_b1", "L3_conv_m1", "L3_conv_be1"),
                                                     ("L3_conv_g2", "L3_conv_b2", "L3_conv_m2", "L3_conv_be2"))):
                    v.tensor_tensor(bnv[:, k:k + 1], col(b), col(mn), ALU.subtract)
                    done(v.tensor_tensor(bninv[:, k:k + 1], bnr[:, k:k + 1], col(gm), ALU.mult))
                    ins = v.scalar_tensor_tensor(out=bnsh[:, k:k + 1], in0=bnv[:, k:k + 1],
                                                 scalar=bninv[:, k:k + 1], in1=col(be),
                                                 op0=ALU.mult, op1=ALU.add)
                ins.then_inc(bn_ready, 1)

            def key_products(j):
                dve.wait_ge(q2_sb, j + 1)
                dve.wait_ge(k2_sb, j + 1)
                for r in range(len(HEX_RUNS)):
                    if r not in POOL_RUNS[j]:
                        ins = key_product(v, j, r)
                ins.then_inc(prod_dve, 1)

            for n in range(SLOTS):
                if n < NATT:
                    maxes(n)
                if n in (5, 7, 9, 11):
                    group_variance((n - 5) // 2)
                if n in (6, 8, 10, 12):
                    group_norm((n - 6) // 2)
                if 1 <= n <= NATT:
                    normalise(n - 1)
                if n == 2:
                    keys0(1)
                if n == 3:
                    values0(1)
                if 4 <= n <= NATT and n % 2 == 0:
                    residual((n - 4) // 2)
                if n == NATT:
                    residual(n // 2 - 1)
                if n in (4, 6, 8, 10):
                    stats((n - 4) // 2)
                if n in V2_SLOTS:
                    key_products(V2_SLOTS.index(n))
                if n == 2:
                    batch_norm_variances()
                if n == PREPARE + 1:
                    prepared()
                if n == 13:
                    batch_norm()
                if n == SLOTS - 1:
                    dve.wait_ge(tables_in["p2"], 16)
                    v.tensor_copy(w1_hi[:, :], table["w1T"]).then_inc(w1_split, 1)
                    dve.wait_ge(w1_split, 1)
                    v.tensor_tensor(w1_lo[:, :], table["w1T"], w1_hi[:, :].bitcast(F32), ALU.subtract)\
                        .then_inc(w1_split, 1)
                    dve.wait_ge(consts, 1)
                    v.tensor_copy(flat(head_cast_r[:, :, :]), flat(head_cast[:, :, :])).then_inc(cast_r, 1)

            dve.wait_ge(hexs_ps, GROUPS)
            sc = duo[:, 0:NB * 128].rearrange("p (k c n) -> p c k n", k=NB, c=2)

            def maxima(c):
                return v.tensor_reduce(smax[:, c, :], sc[:, c, :, :].rearrange("p k n -> p n k"), AX.X, ALU.max)

            def less_maxima(c):
                v.tensor_tensor(sexp[:, c, :, :], sc[:, c, :, :], rep(smax[:, c, :], NB),
                                ALU.subtract).then_inc(hex_shift, 1)

            def sums(c):
                dve.wait_ge(hex_exp, c + 1)
                done(v.tensor_reduce(ssum[:, c, :], sexp[:, c, :, :].rearrange("p k n -> p n k"), AX.X, ALU.add))

            def weights(c):
                done(v.reciprocal(ssum[:, c, :], ssum[:, c, :]))
                v.tensor_tensor(att[:, c, :, :], sexp[:, c, :, :], rep(ssum[:, c, :], NB), ALU.mult)\
                    .then_inc(att_f32, 1)

            def weighted_values(m):
                j, c = UNITS[m]
                dve.wait_ge(cast_ps, m + 1)
                for h in range(2):
                    k0 = 0
                    src = CAST_BANKS[m % 2][h][:, 0:NB * 64].rearrange("p (k a b) -> p k a b", k=NB, b=SIDE)
                    for run in HEX_RUNS:
                        k1 = k0 + len(run)
                        ins = v.tensor_tensor(
                            products[j][:, k0:k1, 128 * h + 64 * c:128 * h + 64 * c + 64]
                            .rearrange("p k (a b) -> p k a b", b=SIDE),
                            src[:, k0:k1, :, :], hexview(v2, j, run, SIDE // 4, SIDE // 2 * h + SIDE // 4 * c),
                            ALU.mult)
                        k0 = k1
                ins.then_inc(avprod_sb, 1)

            done(maxima(0))
            less_maxima(0)
            done(maxima(1))
            sums(0)
            weights(0)
            less_maxima(1)
            dve.wait_ge(att_upper, 1)
            att_lower_halves(v, 0).then_inc(att_lower0, 1)
            sums(1)
            weights(1)
            for m in range(2 * PAIRS):
                weighted_values(m)

            dve.wait_ge(bnrow_ps, 1)
            for i in range(2):
                v.tensor_tensor(c1s[:, i, :], c1[:, i, :], bank[7][:, 0:128], ALU.mult)
            v.tensor_tensor(ctaps[:, :, :, :], ctap,
                            rep(bank[7][:, 128:256], 3).rearrange("p t (r m) -> p r t m", m=32), ALU.mult)\
                .then_inc(taps_ready, 1)

            def layer_norm(n):
                gr = n % 2
                dst, (gain, shift) = (x1, x2)[n // 2], AFFINE[n // 2]
                dve.wait_ge(rstd_sb, n + 1)
                v.scalar_tensor_tensor(out=xhat[:, gr, :], in0=D_BANK[gr], scalar=cb[:, n // 2:n // 2 + 1],
                                       in1=rstd[:, gr, :], op0=ALU.add, op1=ALU.mult).then_inc(xhat_sb, 1)
                dve.wait_ge(xhat_sb, n + 1)
                v.tensor_scalar(dst[:, gr, :], xhat[:, gr, :], col(gain), col(shift), ALU.mult, ALU.add)\
                    .then_inc(ln_out, 1)

            def halves(gr):
                dve.wait_ge(ln_out, gr + 1)
                for i in range(2):
                    own = slice(64 * i, 64 * i + 64)
                    v.tensor_copy(xs[own, gr, i, :], x1[own, gr, :]).then_inc(x_upper, 1)
                for i in range(2):
                    own, other = slice(64 * i, 64 * i + 64), slice(64 - 64 * i, 128 - 64 * i)
                    dve.wait_ge(x_upper, 2 * gr + i + 1)
                    v.tensor_tensor(xs[other, gr, i, :], x1[own, gr, :], xs[own, gr, i, :].bitcast(F32),
                                    ALU.subtract).then_inc(x_lower, 1)

            def relu_ff(gr):
                for h in range(FH):
                    dve.wait_ge(ff_ps, 2 * FH * gr + FH + h + 1)
                    v.tensor_scalar(ffh[:, gr, h, 1, :], bank[FH + h], col("L2_conv_b1", h), 0.0,
                                    ALU.add, ALU.max).then_inc(ff_dve, 1)

            def shifts(c):
                if c >= 2:
                    dve.wait_ge(c2_ps, c - 1)
                for r in range(CONV_BLOCKS):
                    dve.wait_ge(c1_sb, CONV_BLOCKS * c + r + 1)
                    shift(v, c, r, 0)
                    shift(v, c, r, 2).then_inc(shifted, 1)

            def finish(n):
                b, columns = RESULTS[n]
                dve.wait_ge(c3_ps, n + 1)
                done(v.scalar_tensor_tensor(out=x3[:, columns], in0=b, scalar=col("L3_conv_b3"),
                                            in1=x2.rearrange("p g n -> p (g n)")[:, columns],
                                            op0=ALU.add, op1=ALU.add))
                v.tensor_scalar(fin[:, columns], x3[:, columns], 0.0, None, ALU.max).then_inc(fin_sb, 1)

            layer_norm(0)
            halves(0)
            relu_ff(0)
            layer_norm(1)
            halves(1)
            relu_ff(1)
            layer_norm(2)
            shifts(0)
            layer_norm(3)
            shifts(1)
            shifts(2)
            shifts(3)
            for n in range(len(RESULTS)):
                finish(n)

        @block.tensor
        def _(pe):
            mm = nc.tensor.matmul

            def keep_warm(b, n):
                for _ in range(n):
                    mm(b, zeros[:, 0:128], zeros[:, 0:512], start=True, stop=True)

            pe.wait_ge(zeros_ready, 1)
            keep_warm(bank[0], WARM_UP)

            pe.wait_ge(tables_in["p0"], 16)

            def project0(gr):
                if gr:
                    pe.wait_ge(q0_sb, 1)
                    pe.wait_ge(kz0_act, 2)
                    pe.wait_ge(kz0_dve, 2)
                for j in range(2):
                    pe.wait_ge(x_in[2 * gr + j], 16)
                    for n in range(2):
                        ins = mm(L0_BANKS[n][64 * j:64 * j + 64, 0:TOK],
                                 table["wqk0"][:, 64 * n:64 * n + 64], xT[:, 2 * gr + j, :],
                                 start=True, stop=True)
                ins.then_inc(qk0_ps, 1)

            def project0_values(gr):
                pe.wait_ge(tables_in["pv"], 16)
                if gr:
                    pe.wait_ge(v0_sb, 1)
                for j in range(2):
                    for b in range(BLK):
                        ins = mm(L0_BANKS[2][:, (2 * j + b) * 128:(2 * j + b + 1) * 128],
                                 xT[:, 2 * gr + j, b * 128:b * 128 + 128], table["wv0_bd"],
                                 start=True, stop=True)
                ins.then_inc(v0_ps, 1)

            project0(0)
            project0_values(0)

            def scores(n):
                if n >= 3:
                    pe.wait_ge(exp_done, BLK * (n - 2))
                if n < IMAGES:
                    pe.wait_ge(q0_sb, n // 4 + 1)
                    pe.wait_ge(kz0_act, 2 * (n // 4 + 1))
                    pe.wait_ge(kz0_dve, 2 * (n // 4 + 1))
                    q, k = q0[:, n // 4, :], kz0[:, n, :]
                else:
                    m = n - IMAGES
                    pe.wait_ge(q1_sb, m // 2 + 1)
                    pe.wait_ge(k1_sb, 2 * (m // 2 + 1))
                    q, k = q1[:, m // 2, :], kz1[:, m, :]
                for b in range(BLK):
                    ins = mm(S_BANK[n % 3][:, b * TOK:(b + 1) * TOK], q[:, b * 128:b * 128 + 128], k,
                             start=True, stop=True)
                ins.then_inc(scores_ps, 1)

            def transposes(n):
                pe.wait_ge(norm_done, BLK * (n + 1))
                if n >= 2:
                    pe.wait_ge(probT_sb, n - 1)
                for mb in range(BLK):
                    for b in range(BLK):
                        ins = nc.tensor.transpose(T_BANK[n % 2][:, mb * TOK + b * 128:mb * TOK + b * 128 + 128],
                                                  probn[:, n % 2, b, mb * 128:mb * 128 + 128], ident)
                ins.then_inc(probT_ps, 1)

            def attend(p):
                j = p % PAIRS
                pe.wait_ge(probT_sb, 2 * p + 2)
                if p == 0:
                    pe.wait_ge(v0_sb, 2)
                if 0 < p < NATT // 2 - 1:
                    pe.wait_ge(attn_out, p)
                if 0 < p <= PAIRS:
                    pe.wait_ge(gstats_sb, p)
                if p < PAIRS:
                    val = v0
                else:
                    pe.wait_ge(v1_sb, j + 1)
                    val = v1
                for mb in range(BLK):
                    for i in range(2):
                        ins = mm(OUT_BANK[p][64 * i:64 * i + 64, 0:TOK], val[:, 2 * j + mb, 64 * i:64 * i + 64],
                                 probT[:, (2 * p + i) % 4, mb, :], start=mb == 0, stop=mb == BLK - 1)
                ins.then_inc(pv_ps, 1)

            def prepare():
                pe.wait_ge(tables_in["p1"], 16)
                pe.wait_ge(q0_sb, 2)
                mm(W_BANK[0][:, 0:128], table["wv1T_bd"], table["wo1_bd"], start=True, stop=True)
                mm(W_BANK[0][:, 128:129], table["wo1_bd"], col("L1_conv_bv"), start=True, stop=True)\
                    .then_inc(prep_ps, 1)

            def prepare2():
                pe.wait_ge(probT_sb, NATT)
                pe.wait_ge(attn_out, 2 * PAIRS)
                b = PREP_BANK
                mm(b[:, 0:128], table["outw_bd"], centre, start=True, stop=True)
                for h in range(FH):
                    mm(b[:, 128 + h * CH:128 + h * CH + CH], table["w2"][:, h * 128:h * 128 + 128],
                       centre[:, 0:CH], start=True, stop=True)
                for k, name in enumerate(("L2_conv_out_b", "L2_conv_b2")):
                    ins = mm(b[:, 256 + k:257 + k], centre, col(name), start=True, stop=True)
                ins.then_inc(prep2_ps, 1)

            def group_stats(j):
                pe.wait_ge(stats_sb, j + 1)
                mm(O_BANK[:, 0:2], table["pairavg"], mv[:, j, :], start=True, stop=True)
                mm(O_BANK[:, 2:3], table["pairdiff"], mv[:, j, 0:1], start=True, stop=True)\
                    .then_inc(gstats_ps, 1)

            def project1(j):
                pe.wait_ge(h_ready, j + 1)
                if j == 0:
                    pe.wait_ge(prep_sb, 1)
                    pe.wait_ge(kz0_act, 4)
                    pe.wait_ge(kz0_dve, 4)
                else:
                    pe.wait_ge(v1_sb, j)
                mm(W_BANK[0][:, 0:TOK], table["wq1_bd"], hT[:, j, :], start=True, stop=True).then_inc(qkv1_ps, 1)
                if j:
                    pe.wait_ge(k1_sb, 2 * j)
                mm(W_BANK[1][:, 0:TOK], table["wk1_bd"], hT[:, j, :], start=True, stop=True).then_inc(qkv1_ps, 1)

            def project1_values(j):
                pe.wait_ge(q1_sb, j + 1)
                for b in range(BLK):
                    ins = mm(W_BANK[0][:, b * 128:b * 128 + 128],
                             hT[:, j, b * 128:b * 128 + 128], wvo1[:, :], start=True, stop=True)
                ins.then_inc(qkv1_ps, 1)

            def project2(j, k):
                if k == 0:
                    pe.wait_ge(attn_out, PAIRS + j + 1)
                    if j == 0:
                        pe.wait_ge(tables_in["p2"], 16)
                        pe.wait_ge(v1_sb, PAIRS)
                        pe.wait_ge(k1_sb, 2 * PAIRS)
                    if j == 2:
                        pe.wait_ge(exp_done, BLK * NATT)
                    if j == 1:
                        pe.wait_ge(v2_sb, 1)
                    if j == 3:
                        pe.wait_ge(q2_sb, 3)
                if k == 1 and j % 2:
                    pe.wait_ge(k2_sb, j)
                if k == 2 and j < 2:
                    pe.wait_ge(q2_sb, j + 1)
                if k == 2 and j == 3:
                    pe.wait_ge(v2_sb, 3)
                mm(PROJ2[j][k][:, 0:TOK], inT[:, k, :], zT[:, j, :], start=True, stop=True).then_inc(qkv2_ps, 1)

            def head_sums(gr):
                if gr == 0:
                    pe.wait_ge(v2_sb, 2)
                    pe.wait_ge(k2_sb, 2)
                pe.wait_ge(prod_dve, 2 * gr + 2)
                pe.wait_ge(prod_pool, 2 * gr + 2)
                for k0, k1 in ((0, 4), (4, NB)):
                    for h in range(2):
                        for jp in range(2):
                            row = 64 * h + 32 * jp
                            ins = mm(duo[row:row + 32, k0 * 128:k1 * 128], head_sum[:, 16 - 16 * gr:48 - 16 * gr],
                                     products[2 * gr + jp][:, k0:k1, 128 * h:128 * h + 128],
                                     start=gr == 0, stop=gr == GROUPS - 1)
                ins.then_inc(hexs_ps, 1)

            for n in range(SLOTS):
                if n < NATT:
                    scores(n)
                if n == 2:
                    project0(1)
                if n == 3:
                    project0_values(1)
                if n in (5, 7, 9, 11):
                    group_stats((n - 5) // 2)
                if n in (7, 9, 11, 13):
                    project1_values((n - 7) // 2)
                if 2 <= n <= NATT:
                    transposes(n - 2)
                if n == NATT:
                    transposes(n - 1)
                if n == PREPARE:
                    prepare()
                if 4 <= n <= NATT and n % 2 == 0:
                    attend((n - 4) // 2)
                if n == NATT:
                    attend(n // 2 - 1)
                if n in (6, 8, 10, 12):
                    project1((n - 6) // 2)
                if n in QK2_SLOTS:
                    project2(QK2_SLOTS.index(n), 0)
                    project2(QK2_SLOTS.index(n), 1)
                if n == V2_SLOTS[-1]:
                    head_sums(0)
                if n in V2_SLOTS:
                    project2(V2_SLOTS.index(n), 2)
            head_sums(1)

            def cast(m):
                j, c = UNITS[m]
                if m == 0:
                    pe.wait_ge(cast_r, 1)
                    pe.wait_ge(k2_sb, PAIRS)
                    pe.wait_ge(v2_sb, PAIRS)
                    pe.wait_ge(probT_sb, NATT)
                if m >= 2:
                    pe.wait_ge(avprod_sb, m - 1)
                if m == 1:
                    pe.wait_ge(prep2_sb, 1)
                if m in (0, 2):
                    pe.wait_ge((att_lower0, att_lower1)[c], 1)
                for h in range(2):
                    w = head_cast_r[:, 4 * h + 2 * (j % 2) + j // 2, :]
                    for a in (att_hi, att_lo):
                        ins = mm(CAST_BANKS[m % 2][h][:, 0:NB * 64], w, flat(a[:, c, :, :]),
                                 start=a is att_hi, stop=a is att_lo)
                ins.then_inc(cast_ps, 1)

            def centre_input(gr):
                pe.wait_ge(attn_out, 2 * PAIRS)
                pe.wait_ge(probT_sb, NATT)
                mm(D_BANK[gr], centre, zT[:, 2 * gr:2 * gr + 2, :].rearrange("p a b -> p (a b)"),
                   start=True, stop=False)

            def out_single(j):
                o = D_BANK[j // 2][:, TOK * (j % 2):TOK * (j % 2) + TOK]
                pe.wait_ge(avprod_sb, LAST_UNIT[j])
                mm(o, outc[:, :], products[j][:, NB - 1, :], start=False, stop=False)

            def out_sums(j):
                o = D_BANK[j // 2][:, TOK * (j % 2):TOK * (j % 2) + TOK]
                pe.wait_ge(avsum_sb, LAST_UNIT[j])
                for k in range(NB // 2):
                    ins = mm(o, outc[:, :], value_sums[j][:, k, :], start=False,
                             stop=j % 2 == 1 and k == NB // 2 - 1)
                ins.then_inc(av_used, 1)

            def batch_norm_rows():
                pe.wait_ge(bn_ready, 3)
                pe.wait_ge(hex_shift, 2)
                for k in range(2):
                    b = bninv[:, k:k + 1]
                    column = bass.AP(tensor=b.tensor, offset=b.offset, ap=[list(b.ap[0]), [0, 128]])
                    ins = mm(bank[7][:, 128 * k:128 * k + 128], column, ident, start=True, stop=True)
                ins.then_inc(bnrow_ps, 1)

            def variance(n):
                pe.wait_ge(sq_sb, n + 1)
                if n:
                    pe.wait_ge(lnv_sb, n)
                mm(bank[6], table["mean64"], sq[:, n % 2, :], start=True, stop=True).then_inc(var_ps, 1)

            def feed_forward1(gr):
                pe.wait_ge(w1_split, 2)
                pe.wait_ge(stacked, 1)
                for i in range(2):
                    pe.wait_ge(x_lower, 2 * gr + i + 1)
                    for h in range(FH):
                        if gr:
                            pe.wait_ge(ff_act if i == 0 else ff_dve, h + 1)
                        for w in (w1_hi, w1_lo):
                            ins = mm(bank[FH * i + h], w[:, 128 * h:128 * h + 128], xs[:, gr, i, :],
                                     start=w is w1_hi, stop=w is w1_lo)
                        ins.then_inc(ff_ps, 1)

            def feed_forward2(gr):
                for i in range(2):
                    mm(D_BANK[gr], centre_r[:, i, :], xs[:, gr, i, :], start=i == 0, stop=False)
                for h in range(FH):
                    pe.wait_ge(ff_act, 2 * gr + h + 1)
                    pe.wait_ge(ff_dve, 2 * gr + h + 1)
                    for i in range(2):
                        ins = mm(D_BANK[gr][64 * i:64 * i + 64, :], w2c[:, h, :], ffh[:, gr, h, i, :],
                                 start=False, stop=h == FH - 1)
                ins.then_inc(d_ps, 1)

            def conv1(c):
                gr, i = c // 2, c % 2
                pe.wait_ge(ln_out, 3 + gr)
                if c == 0:
                    pe.wait_ge(taps_ready, 1)
                    pe.wait_ge(ff_act, 4)
                    pe.wait_ge(ff_dve, 4)
                mm(bank[c], c1s[:, i, :], x2[:, gr, :], start=True, stop=True).then_inc(c1_ps, 1)

            def conv2(c):
                pe.wait_ge(shifted, CONV_BLOCKS * (c + 1))
                if c == 1:
                    pe.wait_ge(lnv_sb, 4)
                if c >= 2:
                    pe.wait_ge(c2_sb, c - 1)
                for ty in range(3):
                    for r in range(CONV_BLOCKS):
                        ins = mm(bank[7 - c % 2][32 * r:32 * r + 32, :], ctaps[:, r, ty, :],
                                 strips[:, c % 2, r, :, ty:ty + SIDE, :], start=ty == 0, stop=ty == 2)
                ins.then_inc(c2_ps, 1)

            def conv2_last():
                pe.wait_ge(shifted, CONV_BLOCKS * 4)
                for h in range(2):
                    for ty in range(3):
                        for r in range(CONV_BLOCKS):
                            ins = mm(bank[h][32 * r:32 * r + 32, 0:TOK], ctaps[:, r, ty, :],
                                     strips[:, 1, r, h, ty:ty + SIDE, :], start=ty == 0, stop=ty == 2)
                    ins.then_inc(c2_ps, 1)

            def conv3(n, i):
                b, columns = RESULTS[n]
                gr = n > 0
                if i == 0:
                    pe.wait_ge(c2_sb, 2 * gr + 1)
                else:
                    pe.wait_ge(c2_sb, n + gr + 2)
                c2 = c2out.rearrange("p g i n -> p i g n")[:, i, gr, columns.start - 512 * gr:columns.stop - 512 * gr]
                ins = mm(b[64 * i:64 * i + 64, :], table["c3"], c2, start=True, stop=True)
                if i:
                    ins.then_inc(c3_ps, 1)

            centre_input(0)
            centre_input(1)
            prepare2()
            keep_warm(bank[2], WARM_SOFTMAX)
            batch_norm_rows()
            keep_warm(bank[2], WARM_SOFTMAX2)
            cast(0)
            cast(1)
            cast(2)
            cast(3)
            cast(4)
            cast(5)
            out_sums(0)
            cast(6)
            cast(7)
            out_sums(1)
            out_sums(2)
            variance(0)
            out_single(3)
            out_sums(3)
            variance(1)
            feed_forward1(0)
            feed_forward2(0)
            variance(2)
            feed_forward1(1)
            feed_forward2(1)
            conv1(0)
            variance(3)
            conv1(1)
            conv2(0)
            conv1(2)
            conv1(3)
            conv2(1)
            conv2(2)
            conv3(0, 0)
            conv3(0, 1)
            conv2_last()
            conv3(1, 0)
            conv3(1, 1)
            conv3(2, 0)
            conv3(2, 1)


_OUT = "out_dram"


def packed_inputs(inputs):
    import numpy as np

    f = {k: np.asarray(v) for k, v in inputs.items()}
    part = {name: np.zeros((128, n), np.float32) for p in PACKS.values() for name, n in p}

    def diagonal(name, w):
        part[name][0:64, 0:64] = w
        part[name][64:128, 64:128] = w

    for i in range(2):
        for k, w in enumerate(("L0_conv_wq", "L0_conv_wk")):
            part["wqk0"][64 * i:64 * i + 64, 64 * k + 32 * i:64 * k + 32 * i + RC] = f[w]
    for k, b in enumerate(("L0_conv_bq", "L0_conv_bk")):
        for n in range(4):
            part["vcol"][32 * n:32 * n + RC, k] = f[b]
    for name in VEC64:
        part["vcol"][:, COL[name]] = np.concatenate([f[name], f[name]])
    for name in VEC128:
        part["vcol"][:, COL[name]] = f[name]
    for k in range(3):
        b = f["L2_conv_in_proj_b"][CH * k:CH * k + CH]
        part["vcol"][:, COL["in_proj_b"] + k] = np.concatenate([b, b])
    for h in range(FH):
        part["vcol"][:, COL["L2_conv_b1"] + h] = f["L2_conv_b1"][128 * h:128 * h + 128]
    diagonal("wv0_bd", f["L0_conv_wv"])
    diagonal("wq1_bd", f["L1_conv_Wq"])
    diagonal("wk1_bd", f["L1_conv_Wk"])
    diagonal("wv1T_bd", f["L1_conv_Wv"].T)
    diagonal("wo1_bd", f["L1_conv_Wo"])
    diagonal("outw_bd", f["L2_conv_out_w"])
    for k in range(3):
        w = f["L2_conv_in_proj_w"][CH * k:CH * k + CH].T
        for i in range(2):
            part["inT_bd"][64 * i:64 * i + 64, 128 * k + 64 * i:128 * k + 64 * i + 64] = w
    part["w1T"][:, :] = np.concatenate([f["L2_conv_w1"].T] * 2)
    for i in range(2):
        part["c1"][64 * i:64 * i + 64, CM * i:CM * i + CM] = f["L3_conv_w1"][0, 0]
    part["w2"][0:CH, :] = f["L2_conv_w2"]
    part["c3"][:, :] = f["L3_conv_w3"][0, 0]
    for r in range(CONV_BLOCKS):
        for ty in range(3):
            for tx in range(3):
                for g in range(8):
                    at = 32 * (3 * r + ty) + 4 * g
                    m = 32 * r + 4 * g
                    part["ctap"][32 * tx + 4 * g:32 * tx + 4 * g + 4, at:at + 4] = \
                        f["L3_conv_w2"][ty, tx, :, m:m + 4]
    eye = np.eye(128, dtype=np.float32)
    part["ident"][:, :] = eye
    part["pairavg"][:, :] = np.kron(np.eye(64), np.full((2, 2), 0.5))
    part["pairdiff"][:, :] = np.kron(np.eye(64), np.array([[0.5, -0.5], [-0.5, 0.5]]))
    part["mean64"][:, :] = np.kron(np.eye(2), np.full((64, 64), 1.0 / CH))
    part["centre"][:, :] = np.eye(128) - np.kron(np.eye(2), np.full((64, 64), 1.0 / CH))
    part["head_sum"][:, 16:32] = np.kron(np.eye(16), np.ones((HD, 1)))
    arrays = {p: np.concatenate([part[name] for name, _ in parts], axis=1) for p, parts in PACKS.items()}
    x = f["x"].reshape(PAIRS, 2, TOK, CH)
    arrays["xT"] = np.ascontiguousarray(x.transpose(1, 3, 0, 2).reshape(128, PAIRS * TOK))
    return arrays


def kernel(**inputs):
    import numpy as np
    import concourse.bacc as bacc
    from concourse.bass_utils import run_bass_kernel_spmd

    nc = bacc.Bacc("TRN2", target_bir_lowering=False, num_devices=1)
    arrays = packed_inputs(inputs)
    aps = {name: nc.dram_tensor(f"in_{name}", a.shape, F32, kind="ExternalInput").ap()
           for name, a in arrays.items()}
    out = nc.dram_tensor(_OUT, (128, PAIRS * TOK), F32, kind="ExternalOutput").ap()
    build(nc, aps, out)
    r = run_bass_kernel_spmd(nc, [{f"in_{n}": a for n, a in arrays.items()}], core_ids=[0])
    y = np.asarray(r.results[0][_OUT]).reshape(2, CH, PAIRS, TOK)
    return np.ascontiguousarray(y.transpose(2, 0, 3, 1).reshape(IMAGES, SIDE, SIDE, CH))
```
